# Optimizing a Trainium2 kernel written in Bass

```python
import numpy as np
import jax
import jax.numpy as jnp

def _softmax(x, axis=-1):
    return jax.nn.softmax(x, axis=axis)

def _gelu(x):
    return jax.nn.gelu(x, approximate=True)

def _silu(x):
    return jax.nn.silu(x)

def _sigmoid(x):
    return jax.nn.sigmoid(x)

def _layernorm(x, axis=-1, eps=1e-05):
    m = jnp.mean(x, axis=axis, keepdims=True)
    v = jnp.var(x, axis=axis, keepdims=True)
    return (x - m) / jnp.sqrt(v + eps)

def _scatter_add(tgt, idx, src, axis=0):
    return tgt.at[idx].add(src)

def _segment_sum(src, seg, n):
    return jax.ops.segment_sum(src, seg, n)
kernel_name = 'mk_adj_preln_d2_adj_r2_629f88'

def setup_inputs(seed: int=0):
    np.random.seed(seed)
    _w = jnp.asarray

    def _rec_inputs():
        import jax
        import jax.numpy as jnp
        _gk = jax.random.key(seed)
        x = -0.0001538 + 1 * jax.random.normal(jax.random.fold_in(_gk, 1), (128, 128, 384), jnp.float32)
        _w = (1.0 + jnp.arange(128, dtype=jnp.float32)) ** (-0.5)
        _w = _w / _w.mean()
        _pij = jnp.clip(0.03125 * _w[:, None] * _w[None, :], 0.0, 1.0)
        _a = jax.random.uniform(jax.random.fold_in(_gk, 2), (128, 128, 128)) < _pij
        _af = _a.astype(jnp.float32)
        adj = _af
        return (x, adj)
    x, adj = _rec_inputs()

    def _L0_gnn_setup():
        import jax, jax.numpy as jnp
        import numpy as np
        LN_EPS = 1e-12

        def _digcn_forward(hidden_state, adjacency_matrix, Wl, bl, Ws, bs, Wr, br, ln_w, ln_b):
            B, S, D = hidden_state.shape
            temper = jnp.asarray(D, jnp.float32) ** 0.5
            i = jnp.arange(S)
            upper = (i[None, :] > i[:, None]).astype(hidden_state.dtype)
            lower = (i[None, :] < i[:, None]).astype(hidden_state.dtype)

            def layer(h, params):
                wl, b_l, ws, b_s, wr, b_r, g, beta = params
                u = jnp.einsum('bid,bjd->bij', h, h) / temper
                a = jax.nn.softmax(u, axis=-1)
                delta = a * adjacency_matrix
                attn = delta / (jnp.sum(delta, axis=-1, keepdims=True) + 1e-10)
                hl = h @ wl.T + b_l
                hs = h @ ws.T + b_s
                hr = h @ wr.T + b_r
                diag_a = jnp.diagonal(attn, axis1=1, axis2=2)
                ctx = jnp.einsum('bij,bjd->bid', attn * upper, hl) + diag_a[..., None] * hs + jnp.einsum('bij,bjd->bid', attn * lower, hr)
                mean = ctx.mean(-1, keepdims=True)
                var = ctx.var(-1, keepdims=True)
                o = (ctx - mean) / jnp.sqrt(var + LN_EPS) * g + beta
                return (jax.nn.relu(o), None)
            out, _ = jax.lax.scan(layer, hidden_state, (Wl, bl, Ws, bs, Wr, br, ln_w, ln_b))
            return out
        key = jax.random.key(seed)
        ks = jax.random.split(key, 6)
        B, S, D, L = (8, 512, 384, 2)
        scale = (1.0 / D) ** 0.5
        hidden_state = jax.random.normal(ks[0], (B, S, D), jnp.float32)
        adjacency_matrix = (jax.random.uniform(ks[1], (B, S, S)) < 0.05).astype(jnp.float32)
        Wl = jax.random.normal(ks[2], (L, D, D), jnp.float32) * scale
        Ws = jax.random.normal(ks[3], (L, D, D), jnp.float32) * scale
        Wr = jax.random.normal(ks[4], (L, D, D), jnp.float32) * scale
        bl = jnp.zeros((L, D), jnp.float32)
        bs = jnp.zeros((L, D), jnp.float32)
        br = jnp.zeros((L, D), jnp.float32)
        ln_w = jnp.ones((L, D), jnp.float32)
        ln_b = jnp.zeros((L, D), jnp.float32)
        return dict(hidden_state=hidden_state, adjacency_matrix=adjacency_matrix, Wl=Wl, bl=bl, Ws=Ws, bs=bs, Wr=Wr, br=br, ln_w=ln_w, ln_b=ln_b)
    _L0_gnn_all = _L0_gnn_setup()
    _L0_gnn_in = {k: v for k, v in _L0_gnn_all.items() if k in ('Wl', 'bl', 'Ws', 'bs', 'Wr', 'br', 'ln_w', 'ln_b')}
    del _L0_gnn_all

    def _L1_gnn_setup():
        import jax, jax.numpy as jnp
        import numpy as np
        NUM_HEADS = 12
        HIDDEN = 384
        HEAD = HIDDEN // NUM_HEADS
        SCALE = HIDDEN ** (-0.5)
        key = jax.random.key(seed)
        ks = jax.random.split(key, 8)
        B, N = (16, 256)
        std = HIDDEN ** (-0.5)
        return {'x': jax.random.normal(ks[0], (B, N, HIDDEN), dtype=jnp.float32), 'encoding_bias': jax.random.normal(ks[1], (B, N, N), dtype=jnp.float32), 'Wq': jax.random.normal(ks[2], (HIDDEN, HIDDEN), dtype=jnp.float32) * std, 'Wk': jax.random.normal(ks[3], (HIDDEN, HIDDEN), dtype=jnp.float32) * std, 'Wv': jax.random.normal(ks[4], (HIDDEN, HIDDEN), dtype=jnp.float32) * std, 'bv': jax.random.normal(ks[5], (HIDDEN,), dtype=jnp.float32) * 0.01, 'Wo': jax.random.normal(ks[6], (HIDDEN, HIDDEN), dtype=jnp.float32) * std, 'bo': jax.random.normal(ks[7], (HIDDEN,), dtype=jnp.float32) * 0.01}
    _L1_gnn_all = _L1_gnn_setup()
    _L1_gnn_in = {k: v for k, v in _L1_gnn_all.items() if k in ('Wq', 'Wk', 'Wv', 'bv', 'Wo', 'bo')}
    del _L1_gnn_all
    return {'x': x, 'adj': adj, 'L0_gnn_Wl': _L0_gnn_in['Wl'], 'L0_gnn_bl': _L0_gnn_in['bl'], 'L0_gnn_Ws': _L0_gnn_in['Ws'], 'L0_gnn_bs': _L0_gnn_in['bs'], 'L0_gnn_Wr': _L0_gnn_in['Wr'], 'L0_gnn_br': _L0_gnn_in['br'], 'L0_gnn_ln_w': _L0_gnn_in['ln_w'], 'L0_gnn_ln_b': _L0_gnn_in['ln_b'], 'L1_gnn_Wq': _L1_gnn_in['Wq'], 'L1_gnn_Wk': _L1_gnn_in['Wk'], 'L1_gnn_Wv': _L1_gnn_in['Wv'], 'L1_gnn_bv': _L1_gnn_in['bv'], 'L1_gnn_Wo': _L1_gnn_in['Wo'], 'L1_gnn_bo': _L1_gnn_in['bo']}

def reference(x, adj, L0_gnn_Wl, L0_gnn_bl, L0_gnn_Ws, L0_gnn_bs, L0_gnn_Wr, L0_gnn_br, L0_gnn_ln_w, L0_gnn_ln_b, L1_gnn_Wq, L1_gnn_Wk, L1_gnn_Wv, L1_gnn_bv, L1_gnn_Wo, L1_gnn_bo):
    import jax
    import jax.numpy as jnp

    def _L0_gnn_ref(hidden_state, adjacency_matrix, Wl, bl, Ws, bs, Wr, br, ln_w, ln_b):
        import jax, jax.numpy as jnp
        import numpy as np
        LN_EPS = 1e-12

        def _digcn_forward(hidden_state, adjacency_matrix, Wl, bl, Ws, bs, Wr, br, ln_w, ln_b):
            B, S, D = hidden_state.shape
            temper = jnp.asarray(D, jnp.float32) ** 0.5
            i = jnp.arange(S)
            upper = (i[None, :] > i[:, None]).astype(hidden_state.dtype)
            lower = (i[None, :] < i[:, None]).astype(hidden_state.dtype)

            def layer(h, params):
                wl, b_l, ws, b_s, wr, b_r, g, beta = params
                u = jnp.einsum('bid,bjd->bij', h, h) / temper
                a = jax.nn.softmax(u, axis=-1)
                delta = a * adjacency_matrix
                attn = delta / (jnp.sum(delta, axis=-1, keepdims=True) + 1e-10)
                hl = h @ wl.T + b_l
                hs = h @ ws.T + b_s
                hr = h @ wr.T + b_r
                diag_a = jnp.diagonal(attn, axis1=1, axis2=2)
                ctx = jnp.einsum('bij,bjd->bid', attn * upper, hl) + diag_a[..., None] * hs + jnp.einsum('bij,bjd->bid', attn * lower, hr)
                mean = ctx.mean(-1, keepdims=True)
                var = ctx.var(-1, keepdims=True)
                o = (ctx - mean) / jnp.sqrt(var + LN_EPS) * g + beta
                return (jax.nn.relu(o), None)
            out, _ = jax.lax.scan(layer, hidden_state, (Wl, bl, Ws, bs, Wr, br, ln_w, ln_b))
            return out
        return _digcn_forward(hidden_state, adjacency_matrix, Wl, bl, Ws, bs, Wr, br, ln_w, ln_b)

    def _L1_gnn_ref(x, encoding_bias, Wq, Wk, Wv, bv, Wo, bo):
        import jax, jax.numpy as jnp
        import numpy as np
        NUM_HEADS = 12
        HIDDEN = 384
        HEAD = HIDDEN // NUM_HEADS
        SCALE = HIDDEN ** (-0.5)
        B, N, _ = x.shape
        q = (x @ Wq.T).reshape(B, N, NUM_HEADS, HEAD)
        k = (x @ Wk.T).reshape(B, N, NUM_HEADS, HEAD)
        v = (x @ Wv.T + bv).reshape(B, N, NUM_HEADS, HEAD)
        a = jnp.einsum('bnhd,bmhd->bhnm', q, k) * SCALE + encoding_bias[:, None, :, :]
        pad_mask = jnp.all(a == 0, axis=-1)
        a = jnp.where(pad_mask[..., None], -jnp.inf, a)
        a = jax.nn.softmax(a, axis=-1)
        a = jnp.nan_to_num(a)
        o = jnp.einsum('bhnm,bmhd->bnhd', a, v).reshape(B, N, HIDDEN)
        return o @ Wo.T + bo
    h = jnp.maximum(_layernorm(x, axis=-1), 0.0)
    x = x + _L0_gnn_ref(h, adj, L0_gnn_Wl, L0_gnn_bl, L0_gnn_Ws, L0_gnn_bs, L0_gnn_Wr, L0_gnn_br, L0_gnn_ln_w, L0_gnn_ln_b)
    h = jnp.maximum(_layernorm(x, axis=-1), 0.0)
    x = x + _L1_gnn_ref(h, adj, L1_gnn_Wq, L1_gnn_Wk, L1_gnn_Wv, L1_gnn_bv, L1_gnn_Wo, L1_gnn_bo)
    return x

_drawn_inputs = setup_inputs


def setup_inputs(seed=0):
    import zlib

    import numpy as np

    out = dict(_drawn_inputs(seed))
    spreads = {'L0_gnn_bl': (0.0, 0.1),
     'L0_gnn_bs': (0.0, 0.302),
     'L0_gnn_br': (0.0, 0.1),
     'L0_gnn_ln_w': (1.0, 0.2),
     'L0_gnn_ln_b': (0.0, 0.1)}
    factors = {'L1_gnn_Wq': 8.0, 'L1_gnn_Wk': 8.0, 'L1_gnn_bv': 6.743, 'L1_gnn_bo': 7.443}
    for name, (base, spread) in spreads.items():
        noise = np.random.default_rng([zlib.crc32(name.encode()), seed]).standard_normal(out[name].shape)
        drawn = base * np.exp(spread * noise) if base else spread * noise
        out[name] = jnp.asarray(drawn.astype(out[name].dtype))
    for name, factor in factors.items():
        out[name] = (out[name] * factor).astype(out[name].dtype)
    return out
```

```python
from contextlib import ExitStack

import concourse.bass as bass
from concourse import mybir

F32 = mybir.dt.float32
F16 = mybir.dt.float16
I32 = mybir.dt.int32
ALU = mybir.AluOpType
ACT = mybir.ActivationFunctionType
X_AXIS = mybir.AxisListType.X

LN_EPS = 1e-5
DIGCN_EPS = 1e-12
SUM_EPS = 1e-10

H_SCALE = 2.0 ** 10
P_SCALE = 2.0 ** 14
W_TOP = 2.0 ** 14
VAL_SCALE = 2.0 ** -19
SMALLEST = 2.0 ** -30
EXPONENT_BITS = 0x7F800000
LOWEST = -3.0e38


class Graph:

    def __init__(self, pair, parity, last):
        self.pair, self.parity, self.last = pair, parity, last

    def back(self, n):
        p = self.parity - n
        return Graph(self.pair + p // 2, p % 2, self.last)

    def exists(self):
        return not isinstance(self.pair, int) or 0 <= 2 * self.pair + self.parity <= self.last

    def begun(self):
        return not isinstance(self.pair, int) or 2 * self.pair + self.parity >= 0

    def at(self, per, k):
        if isinstance(self.pair, int):
            return per * min(2 * self.pair + self.parity, self.last) + k
        return self.pair * (2 * per) + (per * self.parity + k)

    def loads(self):
        return self.pair * 16 + 16


def two_gnn_blocks(nc, x, adj, w_digcn, b_digcn, ln_w, ln_b, w_mha, bv, bo, out):
    B, S, D = x.shape
    L, W3 = w_digcn.shape[0], w_digcn.shape[1]
    C = D // 128
    H = 12
    HD = D // H
    R = 128 // HD
    SCALE = float(D) ** -0.5
    assert S == 128 and D == C * 128 and W3 == 3 and L == 2 and HD == 32 and B % 2 == 0
    LEFT, SELF, RIGHT = 0, 1, 2
    WQ, WK, WV, WO = 0, 1, 2, 3

    with ExitStack() as ctx:
        def sb(name, shape, dt=F32):
            return ctx.enter_context(nc.sbuf_tensor(name, shape, dt))

        def sem(name):
            return ctx.enter_context(nc.semaphore(name))

        ident = sb("ident", [128, 128])
        side_mask = sb("side_mask", [128, 2, 128])
        wd_raw = sb("wd_raw", [128, L, 3, C, D])
        wm_raw = sb("wm_raw", [128, 4, C, D])
        wd_hi = sb("wd_hi", [128, L, 3, C, D], F16)
        wd_lo = sb("wd_lo", [128, L, 3, C, D], F16)
        wm_hi = sb("wm_hi", [128, 4, C, D], F16)
        wm_lo = sb("wm_lo", [128, 4, C, D], F16)
        bd = sb("bd", [128, L, 3, D])
        lnw = sb("lnw", [128, L, D])
        lnb = sb("lnb", [128, L, D])
        bv_b = sb("bv_b", [128, D])
        bo_b = sb("bo_b", [128, D])
        bounds = sb("bounds", [128, 12])
        bound_all = sb("bound_all", [128, 8])
        need = sb("need", [128, 8])
        pow2 = sb("pow2", [128, 8])
        inv2 = sb("inv2", [128, 8])
        scl = sb("scl", [128, 24])
        half_neg = sb("half_neg", [128, 1])
        col = iter(range(24))
        s_h1, s_w0, s_w1, s_q, s_k, s_v, s_o = [scl[:, c:c + 1] for c in (next(col) for _ in range(7))]
        val0, val1, ratio1, u_scale1, eps0, eps1, val_v, adj_scale, s_scale, out_scale, tmp_a, tmp_b = [
            scl[:, c:c + 1] for c in (next(col) for _ in range(12))]
        w_scale, val_scale, eps_l = (s_w0, s_w1), (val0, val1), (eps0, eps1)

        carrier = sb("carrier", [1, 1])

        x_in = sb("x_in", [128, 2, D])
        adj_in = sb("adj_in", [128, 2, 128])
        h_nat = [sb(f"h_nat{s}", [128, D]) for s in range(3)]
        hT_hi = [sb(f"hT_hi{s}", [128, C, 128], F16) for s in range(3)]
        hT_lo = [sb(f"hT_lo{s}", [128, C, 128], F16) for s in range(3)]
        stats = [sb(f"stats{s}", [128, 6]) for s in range(4)]
        mean_var = [sb(f"mean_var{s}", [128, 2]) for s in range(4)]
        var2 = [sb(f"var2_{s}", [128, 1]) for s in range(4)]
        rstd = [sb(f"rstd{s}", [128, 1]) for s in range(4)]
        row = [sb(f"row{l}", [128, 16]) for l in range(L)]
        e_u = [sb(f"e_u{l}", [128, 128]) for l in range(L)]
        masked = sb("masked", [128, 128])
        diag_junk = sb("diag_junk", [128, 128])
        attn = [sb(f"attn{l}", [128, 128]) for l in range(L)]
        sides = [sb(f"sides{l}", [128, 2, 128]) for l in range(L)]
        sides_hi = [sb(f"sides_hi{l}", [128, 2, 128], F16) for l in range(L)]
        sides_lo = [sb(f"sides_lo{l}", [128, 2, 128], F16) for l in range(L)]
        val = [sb(f"val{l}", [128, 2, D]) for l in range(L)]
        val_hi = [sb(f"val_hi{l}", [128, 2, D], F16) for l in range(L)]
        val_lo = [sb(f"val_lo{l}", [128, 2, D], F16) for l in range(L)]
        self_val = sb("self_val", [128, D])
        ctx_sb = sb("ctx_sb", [128, D])
        ln_t = sb("ln_t", [128, D])
        ln_out = sb("ln_out", [128, D])
        x1 = sb("x1", [128, D])
        x1_bo = sb("x1_bo", [128, 2, D])
        q_hi = sb("q_hi", [128, C, 128], F16)
        q_lo = sb("q_lo", [128, C, 128], F16)
        k_hi = sb("k_hi", [128, C, 128], F16)
        k_lo = sb("k_lo", [128, C, 128], F16)
        v_sb = sb("v_sb", [128, D])
        v_hi = sb("v_hi", [128, H, HD + 1], F16)
        v_lo = sb("v_lo", [128, H, HD + 1], F16)
        adj_s = sb("adj_s", [128, 128])
        score = sb("score", [128, R, C, 128])
        prob = sb("prob", [128, R, C, 128])
        top = sb("top", [128, R, C])
        top_neg = sb("top_neg", [128, R, C])
        fold1 = sb("fold1", [128, H, 64])
        fold2 = sb("fold2", [128, H, 32])
        fold3 = sb("fold3", [128, H, 16])
        score_sum = sb("score_sum", [128, H])
        top_zero = sb("top_zero", [128, H])
        padded = sb("padded", [128, H])
        kept = sb("kept", [128, R, C])
        pT_hi = sb("pT_hi", [128, C, R, 128], F16)
        pT_lo = sb("pT_lo", [128, C, R, 128], F16)
        inv_sum = sb("inv_sum", [128, H])
        inv_kept = sb("inv_kept", [128, H])
        o_nat = sb("o_nat", [128, D])
        oT_hi = sb("oT_hi", [128, C, 128], F16)
        oT_lo = sb("oT_lo", [128, C, 128], F16)
        out_sb = sb("out_sb", [128, 2, D])

        banks = [ctx.enter_context(nc.psum_tensor(f"bank{i}", [128, 512], F32)) for i in range(8)]
        u_bank, t_bank = banks[6], banks[7]
        u_ps, attnT_ps = u_bank[:, 0:128], u_bank[:, 128:256]
        t_ps = t_bank[:, 0:D]
        pv_ps = t_bank[:, 0:H * (HD + 1)]
        val_ps = [(banks[0], banks[2], banks[1]), (banks[5], banks[1], banks[0])]
        ctx_ps = [banks[3], banks[2]]
        q_ps, k_ps, v_ps = banks[4], banks[5], banks[0]
        s_ps = [banks[1], banks[2], banks[3], banks[4]]
        pT_ps = [banks[3], banks[4], banks[5]]

        weights_in, small_in = sem("weights_in"), sem("small_in")
        x_loaded = [sem("x_loaded0"), sem("x_loaded1")]
        adj_loaded = [sem("adj_loaded0"), sem("adj_loaded1")]
        out_stored = [sem("out_stored0"), sem("out_stored1")]
        consts_made, bounds_made, bounds_shared = sem("consts_made"), sem("bounds_made"), sem("bounds_shared")
        scale_step, w_scaled, w_split_hi, w_split_lo = sem("scale_step"), sem("w_scaled"), sem("w_split_hi"), sem("w_split_lo")
        tr_done = [sem(f"tr_done{s}") for s in range(3)]
        u_done = [sem(f"u_done{l}") for l in range(L)]
        val_done = [sem(f"val_done{l}") for l in range(L)]
        attnT_done = [sem(f"attnT_done{l}") for l in range(L)]
        ctx_done = [sem(f"ctx_done{l}") for l in range(L)]
        qk_done, v_done = sem("qk_done"), sem("v_done")
        s_done = sem("s_done")
        pT_done = sem("pT_done")
        pv_done, oT_done, wo_done = sem("pv_done"), sem("oT_done"), sem("wo_done")
        ln0_step = sem("ln0_step")
        soft_step = [sem(f"soft_step{l}") for l in range(L)]
        sides_made = [sem(f"sides_made{l}") for l in range(L)]
        val_made = [sem(f"val_made{l}") for l in range(L)]
        ctx_step = [sem(f"ctx_step{l}") for l in range(L)]
        hT_lo_made = [sem(f"hT_lo_made{s}") for s in range(3)]
        res_step = sem("res_step")
        qk_lo_made, v_made = sem("qk_lo_made"), sem("v_made")
        score_made, top_made = sem("score_made"), sem("top_made")
        pad_step = sem("pad_step")
        pT_lo_made = sem("pT_lo_made")
        o_step = sem("o_step")
        oT_lo_made, out_made = sem("oT_lo_made"), sem("out_made")
        exp_done = [sem(f"exp_done{l}") for l in range(L)]
        sides_hi_made = [sem(f"sides_hi_made{l}") for l in range(L)]
        val_hi_made = [sem(f"val_hi_made{l}") for l in range(L)]
        hT_hi_made = [sem(f"hT_hi_made{s}") for s in range(3)]
        qk_hi_made, v_hi_made = sem("qk_hi_made"), sem("v_hi_made")
        prob_made = sem("prob_made")
        pT_hi_made, oT_hi_made = sem("pT_hi_made"), sem("oT_hi_made")
        rstd_made = [sem(f"rstd_made{s}") for s in range(4)]
        sides_lo_made = [sem(f"sides_lo_made{l}") for l in range(L)]
        val_lo_made = [sem(f"val_lo_made{l}") for l in range(L)]
        adj_scaled, v_lo_made = sem("adj_scaled"), sem("v_lo_made")
        fold_step, x1_bo_made = sem("fold_step"), sem("x1_bo_made")

        block = ctx.enter_context(nc.Block())

        def apart(eng):
            eng.memset(carrier[:, :], 0.0)

        def run_pipeline(eng, step):
            first, last = 2, B // 2 - 1
            for pair in range(first):
                for parity in range(2):
                    step(Graph(pair, parity, B - 1))
            with eng.Fori(first, last) as pair:
                for parity in range(2):
                    step(Graph(pair, parity, B - 1))
            for pair in range(last, last + 2):
                for parity in range(2):
                    step(Graph(pair, parity, B - 1))

        n_weights = 3 * L + 4
        n_small = 5 * L + 2

        @block.sync
        def _(sp):
            def load_x(g):
                i = 2 * g.pair + g.parity
                sp.dma_start(x_in[:, g.parity, :], x[bass.ds(i, 1), :, :].rearrange("a n d -> n (a d)")
                             ).then_inc(x_loaded[g.parity], 16)

            def load_adj(g):
                i = 2 * g.pair + g.parity
                sp.dma_start(adj_in[:, g.parity, :], adj[bass.ds(i, 1), :, :].rearrange("a n m -> n (a m)")
                             ).then_inc(adj_loaded[g.parity], 16)

            for p in range(2):
                load_x(Graph(0, p, B - 1))
                load_adj(Graph(0, p, B - 1))
            for l in range(L):
                for w in range(3):
                    sp.dma_start(wd_raw[:, l, w, :, :],
                                 w_digcn[l, w].rearrange("(c p) e -> p c e", p=128)).then_inc(weights_in, 16)
            for w in range(4):
                sp.dma_start(wm_raw[:, w, :, :],
                             w_mha[w].rearrange("(c p) e -> p c e", p=128)).then_inc(weights_in, 16)

            def step(t):
                g1, g2 = t.back(1), t.back(2)
                nxt, far = t.back(-1), t.back(-2)
                in_loop = not isinstance(t.pair, int)
                if g1.exists() and (in_loop or 2 * nxt.pair + nxt.parity <= B - 1):
                    sp.wait_ge(adj_scaled, g1.at(1, 1))
                    sp.wait_ge(soft_step[1], g1.at(12, 3))
                    load_adj(nxt)
                if g2.exists():
                    sp.wait_ge(out_made, g2.at(1, 1))
                    i = 2 * g2.pair + g2.parity
                    sp.dma_start(out[bass.ds(i, 1), :, :].rearrange("a n d -> n (a d)"),
                                 out_sb[:, g2.parity, :]).then_inc(out_stored[g2.parity], 16)
                if in_loop or 2 * far.pair + far.parity <= B - 1:
                    sp.wait_ge(res_step, t.at(5, 1))
                    load_x(far)

            run_pipeline(sp, step)
            for p in range(2):
                sp.wait_ge(out_stored[p], 16 * (B // 2))

        @block.gpsimd
        def _(pool):
            pool.memset(ident[:, :], 0.0).then_inc(consts_made, 1)
            pool.memset(side_mask[:, :, :], 1.0).then_inc(consts_made, 1)
            pool.memset(v_hi[:, :, :], 1.0).then_inc(consts_made, 1)
            pool.memset(v_lo[:, :, :], 0.0).then_inc(consts_made, 1)
            pool.memset(half_neg[:, :], -0.5).then_inc(consts_made, 1)
            pool.wait_ge(consts_made, 5)
            pool.affine_select(out=ident[:, :], in_=ident[:, :], compare_op=ALU.not_equal, fill=1.0,
                               base=0, pattern=[[-1, 128]], channel_multiplier=1).then_inc(consts_made, 1)
            pool.affine_select(out=side_mask[:, 0, :], in_=side_mask[:, 0, :], compare_op=ALU.is_gt, fill=0.0,
                               base=0, pattern=[[-1, 128]], channel_multiplier=1).then_inc(consts_made, 1)
            pool.affine_select(out=side_mask[:, 1, :], in_=side_mask[:, 1, :], compare_op=ALU.is_gt, fill=0.0,
                               base=0, pattern=[[1, 128]], channel_multiplier=-1).then_inc(consts_made, 1)
            pool.wait_ge(bounds_made, 6)
            pool.partition_all_reduce(bound_all[:, 0:6], bounds[:, 0:6], 128,
                                      bass.bass_isa.ReduceOp.max).then_inc(bounds_shared, 1)

            def rstd_of(s, g, made, per, k):
                pool.wait_ge(made, g.at(per, k))
                pool.tensor_tensor(rstd[s][:, :], var2[s][:, :], half_neg[:, :], ALU.pow).then_inc(rstd_made[s], 1)

            def side_values_lo(l, side, g):
                pool.wait_ge(val_hi_made[l], g.at(2, side + 1))
                if g.back(1).begun():
                    pool.wait_ge(ctx_done[l], g.back(1).at(1, 1))
                pool.tensor_tensor(val_lo[l][:, side, :], val[l][:, side, :], val_hi[l][:, side, :],
                                   ALU.subtract).then_inc(val_lo_made[l], 1)

            def sides_lo_of(l, g):
                pool.wait_ge(sides_hi_made[l], g.at(1, 1))
                if g.back(1).begun():
                    pool.wait_ge(ctx_done[l], g.back(1).at(1, 1))
                pool.tensor_tensor(sides_lo[l][:, :, :], sides[l][:, :, :], sides_hi[l][:, :, :],
                                   ALU.subtract).then_inc(sides_lo_made[l], 1)

            def step(t):
                g1 = t.back(1)
                nxt = t.back(-1)
                if g1.exists():
                    pool.wait_ge(adj_loaded[g1.parity], g1.loads())
                    if g1.back(1).begun():
                        pool.wait_ge(score_made, g1.back(1).at(R, R))
                    pool.tensor_tensor(adj_s[:, :], adj_in[:, g1.parity, :], adj_scale.broadcast_to([128, 128]),
                                       ALU.mult).then_inc(adj_scaled, 1)
                if t.exists():
                    side_values_lo(0, 0, t)
                    side_values_lo(0, 1, t)
                    sides_lo_of(0, t)
                    rstd_of(1, t, ctx_step[0], 7, 4)
                if g1.exists():
                    pool.wait_ge(v_hi_made, g1.at(1, 1))
                    if g1.back(1).begun():
                        pool.wait_ge(pv_done, g1.back(1).at(1, 1))
                    pool.tensor_tensor(v_lo[:, :, 0:HD], v_sb[:, :].rearrange("p (h d) -> p h d", h=H),
                                       v_hi[:, :, 0:HD], ALU.subtract).then_inc(v_lo_made, 1)
                    sc = score[:, :, :, :].rearrange("p r c m -> p (r c) m")
                    pool.wait_ge(score_made, g1.at(R, R))
                    pool.tensor_tensor(fold1[:, :, :], sc[:, :, 0:64], sc[:, :, 64:128], ALU.add).then_inc(fold_step, 1)
                    pool.wait_ge(fold_step, g1.at(3, 1))
                    pool.tensor_tensor(fold2[:, :, :], fold1[:, :, 0:32], fold1[:, :, 32:64], ALU.add).then_inc(fold_step, 1)
                    pool.wait_ge(fold_step, g1.at(3, 2))
                    if g1.back(1).begun():
                        pool.wait_ge(pad_step, g1.back(1).at(4, 1))
                    pool.tensor_tensor(fold3[:, :, :], fold2[:, :, 0:16], fold2[:, :, 16:32], ALU.add).then_inc(fold_step, 1)
                if t.exists():
                    side_values_lo(1, 0, t)
                    if nxt.exists():
                        rstd_of(0, nxt, ln0_step, 4, 3)
                    side_values_lo(1, 1, t)
                    sides_lo_of(1, t)
                    rstd_of(2, t, ctx_step[1], 7, 4)
                    rstd_of(3, t, res_step, 5, 4)
                    if t.back(2).begun():
                        pool.wait_ge(out_made, t.back(2).at(1, 1))
                    pool.tensor_tensor(x1_bo[:, t.parity, :], x1[:, :], bo_b[:, :], ALU.add).then_inc(x1_bo_made, 1)

            rstd_of(0, Graph(0, 0, B - 1), ln0_step, 4, 3)
            run_pipeline(pool, step)

        @block.scalar
        def _(act):
            def bcast(src):
                return src.partition_broadcast(128)
            for l in range(L):
                for w in range(3):
                    act.dma_start(bd[:, l, w, :], bcast(b_digcn[l, w])).then_inc(small_in, 16)
                act.dma_start(lnw[:, l, :], bcast(ln_w[l])).then_inc(small_in, 16)
                act.dma_start(lnb[:, l, :], bcast(ln_b[l])).then_inc(small_in, 16)
            act.dma_start(bv_b[:, :], bcast(bv)).then_inc(small_in, 16)
            act.dma_start(bo_b[:, :], bcast(bo)).then_inc(small_in, 16)
            for n in range(n_weights):
                l, w = divmod(n, 3)
                src, dst = (wd_raw[:, l, w], wd_hi[:, l, w]) if n < 3 * L else (wm_raw[:, n - 3 * L], wm_hi[:, n - 3 * L])
                act.wait_ge(w_scaled, n + 1)
                act.activation(dst, src, ACT.Copy).then_inc(w_split_hi, 1)

            def hT_hi_of(s, g, last_read, per, k):
                act.wait_ge(tr_done[s], g.at(1, 1))
                if g.back(1).begun():
                    act.wait_ge(last_read, g.back(1).at(per, k))
                act.activation(hT_hi[s][:, :, :], t_ps.rearrange("p (c n) -> p c n", c=C), ACT.Relu).then_inc(hT_hi_made[s], 1)

            def graph_exp(l, g):
                act.wait_ge(soft_step[l], g.at(12, 2))
                act.activation(e_u[l][:, :], u_ps, ACT.Exp, bias=row[l][:, 1:2],
                               scale=SCALE / H_SCALE ** 2 if l == 0 else u_scale1,
                               accum_out=row[l][:, 2:3]).then_inc(exp_done[l], 1)

            def side_values_hi(l, side, g):
                act.wait_ge(val_made[l], g.at(3, side + 1))
                if g.back(1).begun():
                    act.wait_ge(ctx_done[l], g.back(1).at(1, 1))
                if g.back(1).begun():
                    act.wait_ge(val_lo_made[l], g.back(1).at(2, side + 1))
                act.activation(val_hi[l][:, side, :], val[l][:, side, :], ACT.Copy).then_inc(val_hi_made[l], 1)

            def sides_hi_of(l, g):
                act.wait_ge(sides_made[l], g.at(1, 1))
                if g.back(1).begun():
                    act.wait_ge(ctx_done[l], g.back(1).at(1, 1))
                if g.back(1).begun():
                    act.wait_ge(sides_lo_made[l], g.back(1).at(1, 1))
                act.activation(sides_hi[l][:, :, :], sides[l][:, :, :], ACT.Copy).then_inc(sides_hi_made[l], 1)

            def head_exps(r, g):
                act.wait_ge(top_made, g.at(R, r + 1))
                if r == 0:
                    if g.back(1).begun():
                        act.wait_ge(pT_done, g.back(1).at(C, C))
                for c in range(C):
                    ins = act.activation(prob[:, r, c, :], score[:, r, c, :], ACT.Exp, bias=top_neg[:, r, c:c + 1])
                ins.then_inc(prob_made, 1)

            def step(t):
                g1, g2, nxt = t.back(1), t.back(2), t.back(-1)
                if t.exists():
                    graph_exp(0, t)
                    side_values_hi(0, 0, t)
                    side_values_hi(0, 1, t)
                    sides_hi_of(0, t)
                if g1.exists():
                    hT_hi_of(2, g1, v_done, 1, 1)
                    for n, (ps, dst, s) in enumerate(((q_ps, q_hi, SCALE * 2.0 ** -15), (k_ps, k_hi, VAL_SCALE))):
                        act.wait_ge(qk_done, g1.at(2, n + 1))
                        if g1.back(1).begun():
                            act.wait_ge(s_done, g1.back(1).at(R, R))
                        act.activation(dst[:, :, :], ps[:, 0:D].rearrange("p (c n) -> p c n", c=C), ACT.Copy,
                                       scale=s).then_inc(qk_hi_made, 1)
                if g2.exists():
                    act.wait_ge(oT_done, g2.at(1, 1))
                    if g2.back(1).begun():
                        act.wait_ge(wo_done, g2.back(1).at(1, 1))
                    act.activation(oT_hi[:, :, :], t_ps.rearrange("p (c n) -> p c n", c=C), ACT.Copy).then_inc(oT_hi_made, 1)
                if g1.exists():
                    act.wait_ge(v_made, g1.at(1, 1))
                    if g1.back(1).begun():
                        act.wait_ge(pv_done, g1.back(1).at(1, 1))
                    if g1.back(1).begun():
                        act.wait_ge(v_lo_made, g1.back(1).at(1, 1))
                    act.activation(v_hi[:, :, 0:HD], v_sb[:, :].rearrange("p (h d) -> p h d", h=H), ACT.Copy).then_inc(v_hi_made, 1)
                if t.exists():
                    hT_hi_of(1, t, val_done[1], 3, 3)
                if g1.exists():
                    head_exps(0, g1)
                    head_exps(1, g1)
                if t.exists():
                    graph_exp(1, t)
                if g1.exists():
                    head_exps(2, g1)
                    head_exps(3, g1)
                if t.exists():
                    side_values_hi(1, 0, t)
                    side_values_hi(1, 1, t)
                    sides_hi_of(1, t)
                    if nxt.exists():
                        hT_hi_of(0, nxt, val_done[0], 3, 3)
                if g1.exists():
                    for b in range(C):
                        act.wait_ge(pT_done, g1.at(C, b + 1))
                        if g1.back(1).begun():
                            act.wait_ge(pv_done, g1.back(1).at(1, 1))
                        act.activation(pT_hi[:, b], pT_ps[b][:, :].rearrange("p (a n) -> p a n", a=R), ACT.Copy,
                                       scale=P_SCALE).then_inc(pT_hi_made, 1)

            hT_hi_of(0, Graph(0, 0, B - 1), val_done[0], 3, 3)
            run_pipeline(act, step)

        @block.vector
        def _(dve):
            steps = [0]

            def own(ins):
                steps[0] += 1
                ins.then_inc(scale_step, 1)
                dve.wait_ge(scale_step, steps[0])

            def absmax(dst, src):
                return dve.tensor_reduce(dst, src, X_AXIS, ALU.max, apply_absolute_value=True)

            dve.wait_ge(weights_in, 16 * n_weights)
            for l in range(L):
                absmax(bounds[:, l:l + 1], wd_raw[:, l].rearrange("p w c e -> p (w c e)")).then_inc(bounds_made, 1)
            for w in range(4):
                absmax(bounds[:, 2 + w:3 + w], wm_raw[:, w].rearrange("p c e -> p (c e)")).then_inc(bounds_made, 1)
            dve.wait_ge(small_in, 16 * n_small)
            for l in range(L):
                absmax(bounds[:, 6 + l:7 + l], bd[:, l].rearrange("p w e -> p (w e)"))
            absmax(bounds[:, 8:9], bv_b[:, :])
            absmax(bounds[:, 9:10], lnw[:, 0, :])
            own(absmax(bounds[:, 10:11], lnb[:, 0, :]))

            def power_of_two(n):
                own(dve.tensor_scalar(need[:, n:n + 1], need[:, n:n + 1], SMALLEST, None, ALU.max))
                own(dve.tensor_scalar(pow2[:, n:n + 1].bitcast(I32), need[:, n:n + 1].bitcast(I32),
                                      EXPONENT_BITS, None, ALU.bitwise_and))
                own(dve.reciprocal(inv2[:, n:n + 1], pow2[:, n:n + 1]))

            own(dve.tensor_tensor(need[:, 6:7], bounds[:, 9:10], bounds[:, 10:11], ALU.add))
            power_of_two(6)
            own(dve.tensor_scalar(s_h1, inv2[:, 6:7], H_SCALE / 2, None, ALU.mult))
            own(dve.tensor_scalar(ratio1, s_h1, 1.0 / (H_SCALE * D), None, ALU.mult))
            dve.wait_ge(bounds_shared, 1)
            own(dve.tensor_copy(need[:, 0:6], bound_all[:, 0:6]))
            own(dve.tensor_scalar(tmp_a, bounds[:, 6:7], 1.0 / D, None, ALU.mult))
            own(dve.tensor_tensor(need[:, 0:1], need[:, 0:1], tmp_a, ALU.max))
            own(dve.tensor_tensor(tmp_a, bounds[:, 7:8], ratio1, ALU.mult))
            own(dve.tensor_tensor(need[:, 1:2], need[:, 1:2], tmp_a, ALU.max))
            own(dve.tensor_scalar(tmp_a, bounds[:, 8:9], 1.0 / D, None, ALU.mult))
            own(dve.tensor_tensor(need[:, 4:5], need[:, 4:5], tmp_a, ALU.max))
            for n, s in enumerate((s_w0, s_w1, s_q, s_k, s_v, s_o)):
                power_of_two(n)
                own(dve.tensor_scalar(s, inv2[:, n:n + 1], W_TOP, None, ALU.mult))
            for n in range(n_weights):
                l, w = divmod(n, 3)
                raw, s = (wd_raw[:, l, w], w_scale[l]) if n < 3 * L else (wm_raw[:, n - 3 * L], (s_q, s_k, s_v, s_o)[n - 3 * L])
                dve.tensor_scalar(raw, raw, s, None, ALU.mult).then_inc(w_scaled, 1)
            own(dve.tensor_scalar(val0, s_w0, H_SCALE * VAL_SCALE, None, ALU.mult))
            own(dve.tensor_scalar(val1, s_w1, VAL_SCALE, None, ALU.mult))
            own(dve.tensor_tensor(val1, val1, s_h1, ALU.mult))
            own(dve.tensor_scalar(val_v, s_v, H_SCALE * VAL_SCALE, None, ALU.mult))
            for l in range(L):
                own(dve.tensor_scalar(tmp_a, val_scale[l], P_SCALE * DIGCN_EPS ** 0.5, None, ALU.mult))
                own(dve.tensor_tensor(eps_l[l], tmp_a, tmp_a, ALU.mult))
            own(dve.tensor_scalar(tmp_a, s_q, 2.0 ** -14, None, ALU.mult))
            own(dve.tensor_tensor(adj_scale, tmp_a, s_k, ALU.mult))
            own(dve.reciprocal(s_scale, adj_scale))
            own(dve.tensor_tensor(tmp_a, s_h1, s_h1, ALU.mult))
            own(dve.reciprocal(tmp_b, tmp_a))
            own(dve.tensor_scalar(u_scale1, tmp_b, SCALE, None, ALU.mult))
            own(dve.tensor_tensor(tmp_a, val_v, s_o, ALU.mult))
            own(dve.reciprocal(out_scale, tmp_a))
            for l in range(L):
                for w in range(3):
                    dve.tensor_scalar(bd[:, l, w, :], bd[:, l, w, :], val_scale[l], None, ALU.mult)
            dve.tensor_scalar(lnw[:, 0, :], lnw[:, 0, :], s_h1, None, ALU.mult)
            dve.tensor_scalar(lnb[:, 0, :], lnb[:, 0, :], s_h1, None, ALU.mult)
            own(dve.tensor_scalar(bv_b[:, :], bv_b[:, :], val_v, None, ALU.mult))
            for n in range(n_weights):
                l, w = divmod(n, 3)
                raw, hi, lo = (wd_raw, wd_hi, wd_lo) if n < 3 * L else (wm_raw, wm_hi, wm_lo)
                i = (slice(None), l, w) if n < 3 * L else (slice(None), n - 3 * L)
                dve.wait_ge(w_split_hi, n + 1)
                dve.tensor_tensor(lo[i], raw[i], hi[i], ALU.subtract).then_inc(w_split_lo, 1)

            def moments(src, s, sm, g, per, k0):
                dve.wait_ge(sm, g.at(per, k0 - 1))
                dve.bn_stats(stats[s][:, :], src).then_inc(sm, 1)
                dve.wait_ge(sm, g.at(per, k0))
                apart(dve)
                dve.bn_aggr(mean_var[s][:, :], stats[s][:, :]).then_inc(sm, 1)
                dve.wait_ge(sm, g.at(per, k0 + 1))

            def outer_var(s, sm):
                dve.tensor_scalar(var2[s][:, :], mean_var[s][:, 1:2], LN_EPS, H_SCALE ** -2, ALU.add,
                                  ALU.mult).then_inc(sm, 1)

            def normalise(src, s, h, sm, g):
                dve.wait_ge(rstd_made[s], g.at(1, 1))
                if g.back(1).begun():
                    dve.wait_ge(tr_done[h], g.back(1).at(1, 1))
                dve.tensor_scalar(h_nat[h][:, :], src, mean_var[s][:, 0:1], rstd[s][:, :], ALU.subtract,
                                  ALU.mult).then_inc(sm, 1)

            def ln0_moments(g):
                dve.wait_ge(x_loaded[g.parity], g.loads())
                dve.bn_stats(stats[0][:, :], x_in[:, g.parity, :]).then_inc(ln0_step, 1)
                dve.wait_ge(ln0_step, g.at(4, 1))
                apart(dve)
                dve.bn_aggr(mean_var[0][:, :], stats[0][:, :]).then_inc(ln0_step, 1)
                dve.wait_ge(ln0_step, g.at(4, 2))
                outer_var(0, ln0_step)

            def hT_lo_of(s, g):
                dve.wait_ge(hT_hi_made[s], g.at(1, 1))
                dve.scalar_tensor_tensor(hT_lo[s][:, :, :], t_ps.rearrange("p (c n) -> p c n", c=C), 0.0,
                                         hT_hi[s][:, :, :], ALU.max, ALU.subtract).then_inc(hT_lo_made[s], 1)

            def graph_softmax(l, g):
                sm, rw = soft_step[l], row[l]
                scale = SCALE / H_SCALE ** 2 if l == 0 else u_scale1
                c = lambda i: rw[:, i:i + 1]
                dve.wait_ge(u_done[l], g.at(1, 1))
                dve.tensor_reduce(c(0), u_ps, X_AXIS, ALU.max, negate=True).then_inc(sm, 1)
                dve.wait_ge(sm, g.at(12, 1))
                dve.tensor_scalar(c(1), c(0), scale, None, ALU.mult).then_inc(sm, 1)
                if l == 0:
                    dve.wait_ge(adj_loaded[g.parity], g.loads())
                dve.wait_ge(exp_done[l], g.at(1, 1))
                dve.tensor_tensor_reduce(masked[:, :], e_u[l][:, :], adj_in[:, g.parity, :], 1.0, 0.0,
                                         ALU.mult, ALU.add, c(3)).then_inc(sm, 1)
                dve.wait_ge(sm, g.at(12, 3))
                dve.scalar_tensor_tensor(c(5), c(3), 0.0, c(3), ALU.is_equal, ALU.add).then_inc(sm, 1)
                dve.tensor_tensor_reduce(diag_junk[:, :], masked[:, :], ident[:, :], 1.0, 0.0,
                                         ALU.mult, ALU.add, c(4)).then_inc(sm, 1)
                dve.wait_ge(sm, g.at(12, 4))
                dve.reciprocal(c(6), c(5)).then_inc(sm, 1)
                dve.scalar_tensor_tensor(c(7), c(2), SUM_EPS, c(3), ALU.mult, ALU.add).then_inc(sm, 1)
                dve.wait_ge(sm, g.at(12, 6))
                if g.back(1).begun():
                    dve.wait_ge(attnT_done[l], g.back(1).at(1, 1))
                dve.tensor_scalar(attn[l][:, :], masked[:, :], c(6), P_SCALE, ALU.mult, ALU.mult).then_inc(sm, 1)
                dve.wait_ge(sm, g.at(12, 7))
                dve.reciprocal(c(8), c(7)).then_inc(sm, 1)
                dve.tensor_scalar(c(9), c(4), c(6), P_SCALE, ALU.mult, ALU.mult).then_inc(sm, 1)
                dve.wait_ge(sm, g.at(12, 9))
                dve.tensor_tensor(c(10), c(3), c(8), ALU.mult).then_inc(sm, 1)
                dve.wait_ge(sm, g.at(12, 11))
                dve.tensor_tensor(c(11), c(10), c(10), ALU.mult).then_inc(sm, 1)

            def side_values(l, side, g):
                dve.wait_ge(val_done[l], g.at(3, side + 1))
                if g.back(1).begun():
                    dve.wait_ge(val_lo_made[l], g.back(1).at(2, side + 1))
                w = (LEFT, RIGHT)[side]
                dve.scalar_tensor_tensor(val[l][:, side, :], val_ps[l][w][:, 0:D], VAL_SCALE, bd[:, l, w, :],
                                         ALU.mult, ALU.add).then_inc(val_made[l], 1)

            def self_values(l, g):
                dve.wait_ge(val_done[l], g.at(3, 3))
                dve.scalar_tensor_tensor(self_val[:, :], val_ps[l][SELF][:, 0:D], VAL_SCALE, bd[:, l, SELF, :],
                                         ALU.mult, ALU.add).then_inc(val_made[l], 1)

            def attn_sides(l, g):
                dve.wait_ge(attnT_done[l], g.at(1, 1))
                if g.back(1).begun():
                    dve.wait_ge(sides_hi_made[l], g.back(1).at(1, 1))
                if g.back(1).begun():
                    dve.wait_ge(sides_lo_made[l], g.back(1).at(1, 1))
                dve.tensor_tensor(sides[l][:, :, :], attnT_ps.unsqueeze(1).broadcast_to([128, 2, 128]),
                                  side_mask[:, :, :], ALU.mult).then_inc(sides_made[l], 1)

            def digcn_moments(l, g):
                sm = ctx_step[l]
                dve.wait_ge(val_made[l], g.at(3, 3))
                dve.wait_ge(ctx_done[l], g.at(1, 1))
                dve.scalar_tensor_tensor(ctx_sb[:, :], self_val[:, :], row[l][:, 9:10], ctx_ps[l][:, 0:D],
                                         ALU.mult, ALU.add).then_inc(sm, 1)
                moments(ctx_sb[:, :], 1 + l, sm, g, 7, 2)
                dve.tensor_scalar(var2[1 + l][:, :], mean_var[1 + l][:, 1:2], row[l][:, 11:12], eps_l[l],
                                  ALU.mult, ALU.add).then_inc(sm, 1)
                dve.scalar_tensor_tensor(ln_t[:, :], ctx_sb[:, :], mean_var[1 + l][:, 0:1], lnw[:, l, :],
                                         ALU.subtract, ALU.mult).then_inc(sm, 1)

            def digcn_norm(l, g):
                sm = ctx_step[l]
                dve.wait_ge(rstd_made[1 + l], g.at(1, 1))
                dve.tensor_tensor(row[l][:, 12:13], rstd[1 + l][:, :], row[l][:, 10:11], ALU.mult).then_inc(sm, 1)
                dve.wait_ge(sm, g.at(7, 6))
                if l == 0:
                    if g.back(1).begun():
                        dve.wait_ge(tr_done[1], g.back(1).at(1, 1))
                dst = h_nat[1] if l == 0 else ln_out
                dve.scalar_tensor_tensor(dst[:, :], ln_t[:, :], row[l][:, 12:13], lnb[:, l, :], ALU.mult,
                                         ALU.add).then_inc(sm, 1)

            def residual(g):
                dve.wait_ge(ctx_step[1], g.at(7, 7))
                if g.back(1).begun():
                    dve.wait_ge(x1_bo_made, g.back(1).at(1, 1))
                dve.scalar_tensor_tensor(x1[:, :], ln_out[:, :], 0.0, x_in[:, g.parity, :], ALU.max,
                                         ALU.add).then_inc(res_step, 1)
                moments(x1[:, :], 3, res_step, g, 5, 2)
                outer_var(3, res_step)

            def qk_lo(n, g):
                ps, hi, lo, s = ((q_ps, q_hi, q_lo, SCALE * 2.0 ** -15), (k_ps, k_hi, k_lo, VAL_SCALE))[n]
                dve.wait_ge(qk_hi_made, g.at(2, n + 1))
                dve.scalar_tensor_tensor(lo[:, :, :], ps[:, 0:D].rearrange("p (c n) -> p c n", c=C), s, hi[:, :, :],
                                         ALU.mult, ALU.subtract).then_inc(qk_lo_made, 1)

            def head_scores(r, g):
                def tops(r):
                    dve.tensor_scalar(top_neg[:, r, :], top[:, r, :], -1.0, None, ALU.mult).then_inc(top_made, 1)

                if r == 0:
                    dve.wait_ge(adj_scaled, g.at(1, 1))
                    if g.back(1).begun():
                        dve.wait_ge(fold_step, g.back(1).at(3, 1))
                    if g.back(1).begun():
                        dve.wait_ge(prob_made, g.back(1).at(R, R))
                if r > 0:
                    dve.wait_ge(score_made, g.at(R, r))
                dve.wait_ge(s_done, g.at(R, r + 1))
                if r == 0:
                    apart(dve)
                else:
                    tops(r - 1)
                for c in range(C):
                    ins = dve.tensor_tensor_reduce(score[:, r, c, :], s_ps[r][:, c * 128:(c + 1) * 128], adj_s[:, :],
                                                   s_scale, LOWEST, ALU.add, ALU.max, top[:, r, c:c + 1])
                ins.then_inc(score_made, 1)
                if r == R - 1:
                    dve.wait_ge(score_made, g.at(R, R))
                    tops(r)

            def pad_rows(g):
                flat = "p r c -> p (r c)"
                dve.wait_ge(fold_step, g.at(3, 3))
                dve.tensor_reduce(score_sum[:, :], fold3[:, :, :], X_AXIS, ALU.add).then_inc(pad_step, 1)
                dve.tensor_scalar(top_zero[:, :], top[:, :, :].rearrange(flat), 0.0, None, ALU.is_equal).then_inc(pad_step, 1)
                dve.wait_ge(pad_step, g.at(4, 2))
                dve.scalar_tensor_tensor(padded[:, :], score_sum[:, :], 0.0, top_zero[:, :], ALU.is_equal,
                                         ALU.mult).then_inc(pad_step, 1)
                dve.wait_ge(pad_step, g.at(4, 3))
                dve.tensor_scalar(kept[:, :, :].rearrange(flat), padded[:, :], -1.0, 1.0, ALU.mult, ALU.add).then_inc(pad_step, 1)

            def pT_lo_of(b, g):
                dve.wait_ge(pT_hi_made, g.at(C, b + 1))
                dve.scalar_tensor_tensor(pT_lo[:, b].rearrange("p a n -> p (a n)"), pT_ps[b][:, :], P_SCALE,
                                         pT_hi[:, b].rearrange("p a n -> p (a n)"), ALU.mult,
                                         ALU.subtract).then_inc(pT_lo_made, 1)

            def head_outputs(g):
                pv = pv_ps.rearrange("p (h d) -> p h d", h=H)
                dve.wait_ge(pv_done, g.at(1, 1))
                dve.reciprocal(inv_sum[:, :].unsqueeze(2), pv[:, :, HD:HD + 1]).then_inc(o_step, 1)
                dve.wait_ge(o_step, g.at(3, 1))
                dve.wait_ge(pad_step, g.at(4, 4))
                dve.tensor_tensor(inv_kept[:, :].rearrange("p (c r) -> p c r", c=C),
                                  inv_sum[:, :].rearrange("p (c r) -> p c r", c=C),
                                  kept[:, :, :].rearrange("p r c -> p c r"), ALU.mult).then_inc(o_step, 1)
                dve.wait_ge(o_step, g.at(3, 2))
                if g.back(1).begun():
                    dve.wait_ge(oT_done, g.back(1).at(1, 1))
                dve.tensor_tensor(o_nat[:, :].rearrange("p (h d) -> p h d", h=H), pv[:, :, 0:HD],
                                  inv_kept[:, :].unsqueeze(2).broadcast_to([128, H, HD]), ALU.mult).then_inc(o_step, 1)

            def step(t):
                g1, g2, nxt = t.back(1), t.back(2), t.back(-1)
                if t.exists():
                    graph_softmax(0, t)
                if g1.exists():
                    normalise(x1[:, :], 3, 2, res_step, g1)
                if t.exists():
                    side_values(0, 0, t)
                    side_values(0, 1, t)
                    attn_sides(0, t)
                if g1.exists():
                    hT_lo_of(2, g1)
                if t.exists():
                    self_values(0, t)
                    digcn_moments(0, t)
                if g1.exists():
                    qk_lo(0, g1)
                if t.exists():
                    digcn_norm(0, t)
                if g1.exists():
                    qk_lo(1, g1)
                if g2.exists():
                    dve.wait_ge(oT_hi_made, g2.at(1, 1))
                    dve.tensor_tensor(oT_lo[:, :, :], t_ps.rearrange("p (c n) -> p c n", c=C), oT_hi[:, :, :],
                                      ALU.subtract).then_inc(oT_lo_made, 1)
                if g1.exists():
                    dve.wait_ge(v_done, g1.at(1, 1))
                    if g1.back(1).begun():
                        dve.wait_ge(v_lo_made, g1.back(1).at(1, 1))
                    dve.scalar_tensor_tensor(v_sb[:, :], v_ps[:, 0:D], VAL_SCALE, bv_b[:, :], ALU.mult,
                                             ALU.add).then_inc(v_made, 1)
                if t.exists():
                    hT_lo_of(1, t)
                if g1.exists():
                    for r in range(R):
                        head_scores(r, g1)
                if t.exists():
                    graph_softmax(1, t)
                    side_values(1, 0, t)
                    if nxt.exists():
                        ln0_moments(nxt)
                    side_values(1, 1, t)
                    if nxt.exists():
                        normalise(x_in[:, nxt.parity, :], 0, 0, ln0_step, nxt)
                if g2.exists():
                    dve.wait_ge(wo_done, g2.at(1, 1))
                    dve.wait_ge(x1_bo_made, g2.at(1, 1))
                    if not isinstance(g2.pair, int) or g2.pair > 0:
                        dve.wait_ge(out_stored[g2.parity], g2.pair * 16)
                    dve.scalar_tensor_tensor(out_sb[:, g2.parity, :], t_ps, out_scale, x1_bo[:, g2.parity, :],
                                             ALU.mult, ALU.add).then_inc(out_made, 1)
                if t.exists():
                    attn_sides(1, t)
                if g1.exists():
                    pad_rows(g1)
                if t.exists():
                    self_values(1, t)
                    digcn_moments(1, t)
                    if nxt.exists():
                        hT_lo_of(0, nxt)
                    digcn_norm(1, t)
                    residual(t)
                if g1.exists():
                    for b in range(C):
                        pT_lo_of(b, g1)
                    head_outputs(g1)

            dve.wait_ge(consts_made, 8)
            g0 = Graph(0, 0, B - 1)
            ln0_moments(g0)
            normalise(x_in[:, 0, :], 0, 0, ln0_step, g0)
            hT_lo_of(0, g0)
            run_pipeline(dve, step)

        @block.tensor
        def _(pe):
            def three(out_ap, a_hi, a_lo, b_hi, b_lo, first, last):
                pe.matmul(out_ap, a_hi, b_hi, start=first, stop=False)
                pe.matmul(out_ap, a_hi, b_lo, start=False, stop=False)
                return pe.matmul(out_ap, a_lo, b_hi, start=False, stop=last)

            def transposes(s, g):
                for c in range(C):
                    ins = pe.transpose(t_ps[:, c * 128:(c + 1) * 128], h_nat[s][:, c * 128:(c + 1) * 128], ident[:, :])
                ins.then_inc(tr_done[s], 1)

            def graph_scores(l, g):
                pe.wait_ge(hT_lo_made[l], g.at(1, 1))
                for c in range(C):
                    hi, lo = hT_hi[l][:, c, :], hT_lo[l][:, c, :]
                    ins = three(u_ps, hi, lo, hi, lo, c == 0, c == C - 1)
                ins.then_inc(u_done[l], 1)

            def node_values(l, w, g):
                for c in range(C):
                    ins = three(val_ps[l][w][:, 0:D], hT_hi[l][:, c, :], hT_lo[l][:, c, :], wd_hi[:, l, w, c, :],
                                wd_lo[:, l, w, c, :], c == 0, c == C - 1)
                ins.then_inc(val_done[l], 1)

            def transpose_attn(l, g):
                pe.wait_ge(soft_step[l], g.at(12, 8))
                pe.transpose(attnT_ps, attn[l][:, :], ident[:, :]).then_inc(attnT_done[l], 1)

            def weigh_values(l, g):
                pe.wait_ge(sides_lo_made[l], g.at(1, 1))
                for side in range(2):
                    pe.wait_ge(val_lo_made[l], g.at(2, side + 1))
                    ins = three(ctx_ps[l][:, 0:D], sides_hi[l][:, side, :], sides_lo[l][:, side, :],
                                val_hi[l][:, side, :], val_lo[l][:, side, :], side == 0, side == 1)
                ins.then_inc(ctx_done[l], 1)

            def step(t):
                g1, g2, nxt = t.back(1), t.back(2), t.back(-1)
                if t.exists():
                    graph_scores(0, t)
                    if t.back(1).begun():
                        pe.wait_ge(val_made[1], t.back(1).at(3, 2))
                    node_values(0, LEFT, t)
                    if t.back(1).begun():
                        pe.wait_ge(val_made[1], t.back(1).at(3, 3))
                    node_values(0, RIGHT, t)
                    transpose_attn(0, t)
                if g1.exists():
                    if g1.back(1).begun():
                        pe.wait_ge(o_step, g1.back(1).at(3, 3))
                    if g1.begun():
                        pe.wait_ge(res_step, g1.at(5, 5))
                    transposes(2, g1)
                if t.exists():
                    if t.back(1).begun():
                        pe.wait_ge(ctx_step[1], t.back(1).at(7, 1))
                    node_values(0, SELF, t)
                    if g1.back(1).begun():
                        pe.wait_ge(pT_lo_made, g1.back(1).at(C, 1))
                    weigh_values(0, t)
                if g1.exists():
                    if g1.begun():
                        pe.wait_ge(hT_lo_made[2], g1.at(1, 1))
                    for n, ps in enumerate((q_ps, k_ps)):
                        if g1.back(1).begun():
                            pe.wait_ge(pT_lo_made, g1.back(1).at(C, 2 + n))
                        for e in range(C):
                            cols = slice(e * 128, (e + 1) * 128)
                            for c in range(C):
                                ins = three(ps[:, cols], wm_hi[:, n, c, cols], wm_lo[:, n, c, cols],
                                            hT_hi[2][:, c, :], hT_lo[2][:, c, :], c == 0, c == C - 1)
                        ins.then_inc(qk_done, 1)
                if g2.exists():
                    if g2.begun():
                        pe.wait_ge(o_step, g2.at(3, 3))
                    if g1.begun():
                        pe.wait_ge(hT_lo_made[2], g1.at(1, 1))
                    for c in range(C):
                        ins = pe.transpose(t_ps[:, c * 128:(c + 1) * 128], o_nat[:, c * 128:(c + 1) * 128], ident[:, :])
                    ins.then_inc(oT_done, 1)
                if g1.exists():
                    pe.wait_ge(val_made[0], t.at(3, 1))
                    for c in range(C):
                        ins = three(v_ps[:, 0:D], hT_hi[2][:, c, :], hT_lo[2][:, c, :], wm_hi[:, WV, c, :],
                                    wm_lo[:, WV, c, :], c == 0, c == C - 1)
                    ins.then_inc(v_done, 1)
                if t.exists():
                    if g2.begun():
                        pe.wait_ge(oT_lo_made, g2.at(1, 1))
                    pe.wait_ge(ctx_step[0], t.at(7, 7))
                    transposes(1, t)
                if g1.exists():
                    if g1.begun():
                        pe.wait_ge(qk_lo_made, g1.at(2, 2))
                    for r in range(R):
                        if r == 0:
                            pe.wait_ge(val_made[0], t.at(3, 2))
                        elif r == 1:
                            pe.wait_ge(val_made[0], t.at(3, 3))
                        elif r == 2:
                            pe.wait_ge(ctx_step[0], t.at(7, 1))
                        else:
                            pe.wait_ge(qk_lo_made, g1.at(2, 1))
                        rows = slice(r * HD, (r + 1) * HD)
                        for c in range(C):
                            ins = three(s_ps[r][:, c * 128:(c + 1) * 128], q_hi[rows, c, :], q_lo[rows, c, :],
                                        k_hi[rows, c, :], k_lo[rows, c, :], True, True)
                        ins.then_inc(s_done, 1)
                if t.exists():
                    graph_scores(1, t)
                    if g1.begun():
                        pe.wait_ge(qk_lo_made, g1.at(2, 2))
                    node_values(1, LEFT, t)
                    if g1.begun():
                        pe.wait_ge(v_made, g1.at(1, 1))
                    node_values(1, RIGHT, t)
                if g2.exists():
                    if g2.begun():
                        pe.wait_ge(oT_lo_made, g2.at(1, 1))
                    pe.wait_ge(hT_lo_made[1], t.at(1, 1))
                    for c in range(C):
                        ins = three(t_ps, oT_hi[:, c, :], oT_lo[:, c, :], wm_hi[:, WO, c, :], wm_lo[:, WO, c, :],
                                    c == 0, c == C - 1)
                    ins.then_inc(wo_done, 1)
                if t.exists():
                    transpose_attn(1, t)
                    if g1.begun():
                        pe.wait_ge(score_made, g1.at(R, 1))
                    node_values(1, SELF, t)
                    if g1.begun():
                        pe.wait_ge(score_made, g1.at(R, 2))
                    weigh_values(1, t)
                    if nxt.exists():
                        pe.wait_ge(ln0_step, nxt.at(4, 4))
                        if g2.begun():
                            pe.wait_ge(out_made, g2.at(1, 1))
                        transposes(0, nxt)
                if g1.exists():
                    for b in range(C):
                        if b < 2:
                            if g1.begun():
                                pe.wait_ge(score_made, g1.at(R, 3 + b))
                        else:
                            pe.wait_ge(val_made[1], t.at(3, 1))
                        for a in range(R):
                            r, c = divmod(b * R + a, C)
                            if c == 0:
                                if g1.begun():
                                    pe.wait_ge(prob_made, g1.at(R, r + 1))
                            ins = pe.transpose(pT_ps[b][:, a * 128:(a + 1) * 128], prob[:, r, c, :], ident[:, :])
                        ins.then_inc(pT_done, 1)
                    if g1.begun():
                        pe.wait_ge(v_lo_made, g1.at(1, 1))
                    pe.wait_ge(hT_lo_made[0], nxt.at(1, 1))
                    for b in range(C):
                        if g1.begun():
                            pe.wait_ge(pT_lo_made, g1.at(C, b + 1))
                        for a in range(R):
                            r, c = divmod(b * R + a, C)
                            h = c * R + r
                            ins = three(pv_ps[:, h * (HD + 1):(h + 1) * (HD + 1)], pT_hi[:, b, a, :], pT_lo[:, b, a, :],
                                        v_hi[:, h, :], v_lo[:, h, :], True, True)
                    ins.then_inc(pv_done, 1)

            pe.wait_ge(consts_made, 8)
            pe.wait_ge(ln0_step, 4)
            transposes(0, Graph(0, 0, B - 1))
            pe.wait_ge(w_split_lo, n_weights)
            run_pipeline(pe, step)


_OUT = ((128, 128, 384), "float32")


def kernel(**inputs):
    import numpy as _np
    import concourse.bacc as _bacc
    from concourse import mybir as _mybir
    from concourse.bass_utils import run_bass_kernel_spmd as _run

    a = {k: _np.asarray(v) for k, v in inputs.items()}
    arrays = {
        "x": a["x"],
        "adj": a["adj"],
        "w_digcn": _np.stack([a["L0_gnn_Wl"], a["L0_gnn_Ws"], a["L0_gnn_Wr"]], axis=1).transpose(0, 1, 3, 2),
        "b_digcn": _np.stack([a["L0_gnn_bl"], a["L0_gnn_bs"], a["L0_gnn_br"]], axis=1),
        "ln_w": a["L0_gnn_ln_w"],
        "ln_b": a["L0_gnn_ln_b"],
        "w_mha": _np.stack([a["L1_gnn_Wq"], a["L1_gnn_Wk"], a["L1_gnn_Wv"], a["L1_gnn_Wo"]]).transpose(0, 2, 1),
        "bv": a["L1_gnn_bv"],
        "bo": a["L1_gnn_bo"],
    }
    arrays = {f"in_{k}": _np.ascontiguousarray(v) for k, v in arrays.items()}
    nc = _bacc.Bacc("TRN2", target_bir_lowering=False, num_devices=1)
    args = [nc.dram_tensor(k, v.shape, _mybir.dt.from_np(v.dtype), kind="ExternalInput").ap() for k, v in arrays.items()]
    shape, dtype = _OUT
    res = nc.dram_tensor("out_0", shape, _mybir.dt.from_np(_np.dtype(dtype)), kind="ExternalOutput").ap()
    two_gnn_blocks(nc, *args, res)
    r = _run(nc, [arrays], core_ids=[0])
    return r.results[0]["out_0"]
```

```python
from contextlib import ExitStack

import concourse.bass as bass
from concourse import mybir

F32 = mybir.dt.float32
F16 = mybir.dt.float16
I32 = mybir.dt.int32
ALU = mybir.AluOpType
ACT = mybir.ActivationFunctionType
X_AXIS = mybir.AxisListType.X

LN_EPS = 1e-5
DIGCN_EPS = 1e-12
SUM_EPS = 1e-10

H_SCALE = 2.0 ** 10
P_SCALE = 2.0 ** 14
W_TOP = 2.0 ** 14
VAL_SCALE = 2.0 ** -19
SMALLEST = 2.0 ** -30
EXPONENT_BITS = 0x7F800000
HIGHEST = 3.0e38


class Graph:

    def __init__(self, pair, parity, last):
        self.pair, self.parity, self.last = pair, parity, last

    def back(self, n):
        p = self.parity - n
        return Graph(self.pair + p // 2, p % 2, self.last)

    def exists(self):
        return not isinstance(self.pair, int) or 0 <= 2 * self.pair + self.parity <= self.last

    def first(self):
        return isinstance(self.pair, int) and 2 * self.pair + self.parity == 0

    def begun(self):
        return not isinstance(self.pair, int) or 2 * self.pair + self.parity >= 0

    def at(self, per, k):
        if isinstance(self.pair, int):
            return per * min(2 * self.pair + self.parity, self.last) + k
        return self.pair * (2 * per) + (per * self.parity + k)

    def loads(self):
        return self.pair * 16 + 16


def two_gnn_blocks(nc, x, adj, w_digcn, b_digcn, ln_w, ln_b, w_mha, bv, bo, out):
    B, S, D = x.shape
    L, W3 = w_digcn.shape[0], w_digcn.shape[1]
    C = D // 128
    H = 12
    HD = D // H
    R = 128 // HD
    SCALE = float(D) ** -0.5
    assert S == 128 and D == C * 128 and W3 == 3 and L == 2 and HD == 32 and B % 2 == 0
    LEFT, SELF, RIGHT = 0, 1, 2
    WQ, WK, WV, WO = 0, 1, 2, 3

    with ExitStack() as ctx:
        def sb(name, shape, dt=F32):
            return ctx.enter_context(nc.sbuf_tensor(name, shape, dt))

        def sem(name):
            return ctx.enter_context(nc.semaphore(name))

        ident = sb("ident", [128, 128])
        side_mask = sb("side_mask", [128, 2, 128])
        wd_raw = sb("wd_raw", [128, L, 3, C, D])
        wm_raw = sb("wm_raw", [128, 4, C, D])
        wd_hi = sb("wd_hi", [128, L, 3, C, D], F16)
        wd_lo = sb("wd_lo", [128, L, 3, C, D], F16)
        wm_hi = sb("wm_hi", [128, 4, C, D], F16)
        wm_lo = sb("wm_lo", [128, 4, C, D], F16)
        bd = sb("bd", [128, L, 3, D])
        lnw = sb("lnw", [128, L, D])
        lnb = sb("lnb", [128, L, D])
        bv_b = sb("bv_b", [128, D])
        bo_b = sb("bo_b", [128, D])
        bounds = sb("bounds", [128, 3 * L + 4])
        bound_all = sb("bound_all", [128, 3 * L + 4])
        need = sb("need", [128, L + 4])
        least = sb("least", [128, L + 4])
        pow2 = sb("pow2", [128, L + 4])
        inv2 = sb("inv2", [128, L + 4])
        h_need = sb("h_need", [128, 1])
        bias_max = sb("bias_max", [128, 5])
        scl = sb("scl", [128, 24])
        half_neg = sb("half_neg", [128, 1])
        col = iter(range(24))
        s_w0, s_w1, s_q, s_k, s_v, s_o, s_h1 = [scl[:, c:c + 1] for c in (next(col) for _ in range(7))]
        val0, val1, ratio1, u_scale1, eps0, eps1, val_v, adj_scale, s_scale_neg, out_scale, tmp_a, tmp_b = [
            scl[:, c:c + 1] for c in (next(col) for _ in range(12))]
        w_scale, val_scale, eps_l = (s_w0, s_w1), (val0, val1), (eps0, eps1)

        carrier = sb("carrier", [1, 8])

        x_in = sb("x_in", [128, 2, D])
        adj_in = sb("adj_in", [128, 2, 128])
        h_nat = [sb(f"h_nat{s}", [128, D]) for s in range(3)]
        hT_hi = [sb(f"hT_hi{s}", [128, C, 128], F16) for s in range(3)]
        hT_lo = [sb(f"hT_lo{s}", [128, C, 128], F16) for s in range(3)]
        stats = [sb(f"stats{s}", [128, 6]) for s in range(4)]
        mean_var = [sb(f"mean_var{s}", [128, 2]) for s in range(4)]
        var2 = [sb(f"var2_{s}", [128, 1]) for s in range(4)]
        rstd = [sb(f"rstd{s}", [128, 1]) for s in range(4)]
        row = [sb(f"row{l}", [128, 16]) for l in range(L)]
        e_u = [sb(f"e_u{l}", [128, 128]) for l in range(L)]
        masked = [sb(f"masked{l}", [128, 128]) for l in range(L)]
        diag_junk = [sb(f"diag_junk{l}", [128, 128]) for l in range(L)]
        attn = [sb(f"attn{l}", [128, 128]) for l in range(L)]
        sides = [sb(f"sides{l}", [128, 2, 128]) for l in range(L)]
        sides_hi = [sb(f"sides_hi{l}", [128, 2, 128], F16) for l in range(L)]
        sides_lo = [sb(f"sides_lo{l}", [128, 2, 128], F16) for l in range(L)]
        val = [sb(f"val{l}", [128, 2, D]) for l in range(L)]
        val_hi = [sb(f"val_hi{l}", [128, 2, D], F16) for l in range(L)]
        val_lo = [sb(f"val_lo{l}", [128, 2, D], F16) for l in range(L)]
        self_raw = [sb(f"self_raw{l}", [128, D]) for l in range(L)]
        self_val = [sb(f"self_val{l}", [128, D]) for l in range(L)]
        ctx_sb = [sb(f"ctx_sb{l}", [128, D]) for l in range(L)]
        ln_t = [sb(f"ln_t{l}", [128, D]) for l in range(L)]
        ln_out = sb("ln_out", [128, D])
        x1 = sb("x1", [128, D])
        x1_bo = sb("x1_bo", [128, 2, D])
        q_hi = sb("q_hi", [128, C, 128], F16)
        q_lo = sb("q_lo", [128, C, 128], F16)
        k_hi = sb("k_hi", [128, C, 128], F16)
        k_lo = sb("k_lo", [128, C, 128], F16)
        v_sb = sb("v_sb", [128, D])
        v_hi = sb("v_hi", [128, H, HD + 1], F16)
        v_lo = sb("v_lo", [128, H, HD + 1], F16)
        adj_s = sb("adj_s", [128, 128])
        score_neg = sb("score_neg", [128, R, C, 128])
        prob = sb("prob", [128, R, C, 128])
        top_neg = sb("top_neg", [128, R, C])
        fold1 = sb("fold1", [128, H, 64])
        fold2 = sb("fold2", [128, H, 32])
        fold3 = sb("fold3", [128, H, 16])
        score_sum = sb("score_sum", [128, H])
        top_nonzero = sb("top_nonzero", [128, H])
        kept = sb("kept", [128, R, C])
        pT = sb("pT", [128, C, R * 128])
        pT_hi = sb("pT_hi", [128, C, R, 128], F16)
        pT_lo = sb("pT_lo", [128, C, R, 128], F16)
        inv_sum = sb("inv_sum", [128, H])
        inv_kept = sb("inv_kept", [128, H])
        o_nat = sb("o_nat", [128, D])
        oT_hi = sb("oT_hi", [128, C, 128], F16)
        oT_lo = sb("oT_lo", [128, C, 128], F16)
        out_raw = sb("out_raw", [128, D])
        out_sb = sb("out_sb", [128, 2, D])

        banks = [ctx.enter_context(nc.psum_tensor(f"bank{i}", [128, 512], F32)) for i in range(8)]
        u_ps = [banks[3][:, 0:128], banks[7][:, 0:128]]
        attnT_ps = [banks[1][:, 0:128], banks[0][:, 0:128]]
        val_ps = [(banks[2], banks[6], banks[6]), (banks[5], banks[7], banks[4])]
        ctx_ps = [banks[5], banks[2]]
        t_ps = [banks[3][:, 0:D], banks[7][:, 0:D], banks[4][:, 0:D]]
        q_ps, k_ps, v_ps = banks[0], banks[5], banks[7]
        s_ps = [banks[0], banks[1], banks[1], banks[5]]
        pT_ps = [banks[2], banks[4], banks[2]]
        pv_ps = banks[5][:, 0:H * (HD + 1)]
        oT_ps = banks[6][:, 0:D]
        wo_ps = banks[6][:, 0:D]

        n_weights = 3 * L + 4
        n_small = 5 * L + 2
        weight_in, small_in = [sem(f"weight_in{n}") for n in range(n_weights)], sem("small_in")
        x_loaded = [sem("x_loaded0"), sem("x_loaded1")]
        adj_loaded = [sem("adj_loaded0"), sem("adj_loaded1")]
        out_stored = [sem("out_stored0"), sem("out_stored1")]
        consts_made, bounds_made, bounds_shared = sem("consts_made"), sem("bounds_made"), sem("bounds_shared")
        scale_step, scales_made, prepared = sem("scale_step"), sem("scales_made"), sem("prepared")
        w_split_hi, w_split_lo = sem("w_split_hi"), sem("w_split_lo")
        tr_done = [sem(f"tr_done{s}") for s in range(3)]
        u_done = [sem(f"u_done{l}") for l in range(L)]
        val_done = [[sem(f"val_done{l}{w}") for w in range(3)] for l in range(L)]
        attnT_done = [sem(f"attnT_done{l}") for l in range(L)]
        ctx_done = [sem(f"ctx_done{l}") for l in range(L)]
        qk_done, v_done = sem("qk_done"), sem("v_done")
        s_done = sem("s_done")
        pT_done = sem("pT_done")
        pv_done, oT_done, wo_done = sem("pv_done"), sem("oT_done"), sem("wo_done")
        ln0_step = sem("ln0_step")
        soft_step = [sem(f"soft_step{l}") for l in range(L)]
        sides_made = [sem(f"sides_made{l}") for l in range(L)]
        val_made = [sem(f"val_made{l}") for l in range(L)]
        ctx_step = [sem(f"ctx_step{l}") for l in range(L)]
        hT_lo_made = [sem(f"hT_lo_made{s}") for s in range(3)]
        res_step = sem("res_step")
        qk_lo_made, v_made = sem("qk_lo_made"), sem("v_made")
        score_made = sem("score_made")
        pad_step = sem("pad_step")
        o_step = sem("o_step")
        oT_lo_made = sem("oT_lo_made")
        exp_done = [sem(f"exp_done{l}") for l in range(L)]
        sides_hi_made = [sem(f"sides_hi_made{l}") for l in range(L)]
        val_hi_made = [sem(f"val_hi_made{l}") for l in range(L)]
        hT_hi_made = [sem(f"hT_hi_made{s}") for s in range(3)]
        qk_hi_made, v_hi_made = sem("qk_hi_made"), sem("v_hi_made")
        prob_made = sem("prob_made")
        self_copied = [sem(f"self_copied{l}") for l in range(L)]
        pT_hi_made, pT_copied = sem("pT_hi_made"), sem("pT_copied")
        oT_hi_made, out_scaled = sem("oT_hi_made"), sem("out_scaled")
        rstd_made = [sem(f"rstd_made{s}") for s in range(4)]
        sides_lo_made = [sem(f"sides_lo_made{l}") for l in range(L)]
        val_lo_made = [sem(f"val_lo_made{l}") for l in range(L)]
        adj_scaled, v_lo_made = sem("adj_scaled"), sem("v_lo_made")
        fold_step, x1_bo_made = sem("fold_step"), sem("x1_bo_made")
        self_made = [sem(f"self_made{l}") for l in range(L)]
        pT_lo_made, out_made = sem("pT_lo_made"), sem("out_made")

        block = ctx.enter_context(nc.Block())

        def weight(wd, wm, n):
            return wd[:, n // 3, n % 3] if n < 3 * L else wm[:, n - 3 * L]

        def scale_of(n):
            return w_scale[n // 3] if n < 3 * L else (s_q, s_k, s_v, s_o)[n - 3 * L]

        def apart(eng, n):
            eng.memset(carrier[:, n:n + 1], 0.0)

        def run_pipeline(eng, step):
            first, last = 2, B // 2 - 1
            for pair in range(first):
                for parity in range(2):
                    step(Graph(pair, parity, B - 1))
            with eng.Fori(first, last) as pair:
                for parity in range(2):
                    step(Graph(pair, parity, B - 1))
            for pair in range(last, last + 2):
                for parity in range(2):
                    step(Graph(pair, parity, B - 1))

        def load_small(eng, half):
            pairs = [(bd[:, l, w, :], b_digcn[l, w]) for l in range(L) for w in range(3)]
            pairs += [(lnw[:, l, :], ln_w[l]) for l in range(L)] + [(lnb[:, l, :], ln_b[l]) for l in range(L)]
            pairs += [(bv_b[:, :], bv), (bo_b[:, :], bo)]
            for dst, src in pairs[half::2]:
                eng.dma_start(dst, src.partition_broadcast(128)).then_inc(small_in, 16)

        @block.sync
        def _(sp):
            def load_x(g):
                i = 2 * g.pair + g.parity
                sp.dma_start(x_in[:, g.parity, :], x[bass.ds(i, 1), :, :].rearrange("a n d -> n (a d)")
                             ).then_inc(x_loaded[g.parity], 16)

            def load_adj(g):
                i = 2 * g.pair + g.parity
                sp.dma_start(adj_in[:, g.parity, :], adj[bass.ds(i, 1), :, :].rearrange("a n m -> n (a m)")
                             ).then_inc(adj_loaded[g.parity], 16)

            load_x(Graph(0, 0, B - 1))
            load_adj(Graph(0, 0, B - 1))
            load_small(sp, 0)
            for l in range(L):
                for w in range(3):
                    sp.dma_start(wd_raw[:, l, w, :, :],
                                 w_digcn[l, w].rearrange("(c p) e -> p c e", p=128)).then_inc(weight_in[3 * l + w], 16)
            for w in range(4):
                sp.dma_start(wm_raw[:, w, :, :],
                             w_mha[w].rearrange("(c p) e -> p c e", p=128)).then_inc(weight_in[3 * L + w], 16)

            def step(t):
                g1, g2, nxt = t.back(1), t.back(2), t.back(-1)
                if nxt.exists():
                    if g1.begun():
                        sp.wait_ge(res_step, g1.at(5, 1))
                    load_x(nxt)
                    if g1.begun():
                        sp.wait_ge(adj_scaled, g1.at(1, 1))
                        sp.wait_ge(soft_step[1], g1.at(10, 3))
                    load_adj(nxt)
                if g2.exists():
                    sp.wait_ge(out_made, g2.at(1, 1))
                    i = 2 * g2.pair + g2.parity
                    sp.dma_start(out[bass.ds(i, 1), :, :].rearrange("a n d -> n (a d)"),
                                 out_sb[:, g2.parity, :]).then_inc(out_stored[g2.parity], 16)

            run_pipeline(sp, step)
            for p in range(2):
                sp.wait_ge(out_stored[p], 16 * (B // 2))

        @block.gpsimd
        def _(pool):
            pool.memset(ident[:, :], 0.0).then_inc(consts_made, 1)
            pool.memset(side_mask[:, :, :], 1.0).then_inc(consts_made, 1)
            pool.memset(v_hi[:, :, :], 1.0).then_inc(consts_made, 1)
            pool.memset(v_lo[:, :, :], 0.0).then_inc(consts_made, 1)
            pool.memset(half_neg[:, :], -0.5).then_inc(consts_made, 1)
            pool.memset(least[:, :], SMALLEST).then_inc(consts_made, 1)
            pool.wait_ge(consts_made, 6)
            pool.affine_select(out=ident[:, :], in_=ident[:, :], compare_op=ALU.not_equal, fill=1.0,
                               base=0, pattern=[[-1, 128]], channel_multiplier=1).then_inc(consts_made, 1)
            pool.affine_select(out=side_mask[:, 0, :], in_=side_mask[:, 0, :], compare_op=ALU.is_gt, fill=0.0,
                               base=0, pattern=[[-1, 128]], channel_multiplier=1).then_inc(consts_made, 1)
            pool.affine_select(out=side_mask[:, 1, :], in_=side_mask[:, 1, :], compare_op=ALU.is_gt, fill=0.0,
                               base=0, pattern=[[1, 128]], channel_multiplier=-1).then_inc(consts_made, 1)
            def rstd_of(s, g, made, per, k):
                pool.wait_ge(made, g.at(per, k))
                pool.tensor_tensor(rstd[s][:, :], var2[s][:, :], half_neg[:, :], ALU.pow).then_inc(rstd_made[s], 1)

            def side_values_lo(l, side, g):
                pool.wait_ge(val_hi_made[l], g.at(2, side + 1))
                if g.back(1).begun():
                    pool.wait_ge(ctx_done[l], g.back(1).at(1, 1))
                pool.tensor_tensor(val_lo[l][:, side, :], val[l][:, side, :], val_hi[l][:, side, :],
                                   ALU.subtract).then_inc(val_lo_made[l], 1)

            def sides_lo_of(l, g):
                pool.wait_ge(sides_hi_made[l], g.at(1, 1))
                if g.back(1).begun():
                    pool.wait_ge(ctx_done[l], g.back(1).at(1, 1))
                pool.tensor_tensor(sides_lo[l][:, :, :], sides[l][:, :, :], sides_hi[l][:, :, :],
                                   ALU.subtract).then_inc(sides_lo_made[l], 1)

            def self_bias(l, g):
                pool.wait_ge(self_copied[l], g.at(1, 1))
                if g.back(1).begun():
                    pool.wait_ge(ctx_step[l], g.back(1).at(7, 1))
                pool.tensor_tensor(self_val[l][:, :], self_raw[l][:, :], bd[:, l, SELF, :],
                                   ALU.add).then_inc(self_made[l], 1)

            def probs_lo(b, g):
                pool.wait_ge(pT_copied, g.at(C, b + 1))
                if g.back(1).begun():
                    pool.wait_ge(pv_done, g.back(1).at(1, 1))
                pool.tensor_tensor(pT_lo[:, b].rearrange("p a n -> p (a n)"), pT[:, b, :],
                                   pT_hi[:, b].rearrange("p a n -> p (a n)"), ALU.subtract).then_inc(pT_lo_made, 1)

            def scale_adj(g):
                pool.wait_ge(adj_loaded[g.parity], g.loads())
                if g.back(1).begun():
                    pool.wait_ge(score_made, g.back(1).at(R, R))
                pool.tensor_tensor(adj_s[:, :], adj_in[:, g.parity, :], adj_scale.broadcast_to([128, 128]),
                                   ALU.mult).then_inc(adj_scaled, 1)

            def residual_and_bias(g):
                pool.wait_ge(res_step, g.at(5, 1))
                if g.back(2).begun():
                    pool.wait_ge(out_made, g.back(2).at(1, 1))
                pool.tensor_tensor(x1_bo[:, g.parity, :], x1[:, :], bo_b[:, :], ALU.add).then_inc(x1_bo_made, 1)

            def output(g):
                pool.wait_ge(out_scaled, g.at(1, 1))
                if not isinstance(g.pair, int) or g.pair > 0:
                    pool.wait_ge(out_stored[g.parity], g.pair * 16)
                pool.tensor_tensor(out_sb[:, g.parity, :], out_raw[:, :], x1_bo[:, g.parity, :],
                                   ALU.add).then_inc(out_made, 1)

            def v_lo_of(g):
                pool.wait_ge(v_hi_made, g.at(1, 1))
                if g.back(1).begun():
                    pool.wait_ge(pv_done, g.back(1).at(1, 1))
                pool.tensor_tensor(v_lo[:, :, 0:HD], v_sb[:, :].rearrange("p (h d) -> p h d", h=H),
                                   v_hi[:, :, 0:HD], ALU.subtract).then_inc(v_lo_made, 1)

            def fold_scores(g):
                sc = score_neg[:, :, :, :].rearrange("p r c m -> p (r c) m")
                pool.wait_ge(score_made, g.at(R, R))
                pool.tensor_tensor(fold1[:, :, :], sc[:, :, 0:64], sc[:, :, 64:128], ALU.add).then_inc(fold_step, 1)

            def fold_again(g):
                pool.wait_ge(fold_step, g.at(3, 1))
                pool.tensor_tensor(fold2[:, :, :], fold1[:, :, 0:32], fold1[:, :, 32:64], ALU.add).then_inc(fold_step, 1)

            def fold_last(g):
                pool.wait_ge(fold_step, g.at(3, 2))
                if g.back(1).begun():
                    pool.wait_ge(pad_step, g.back(1).at(3, 1))
                pool.tensor_tensor(fold3[:, :, :], fold2[:, :, 0:16], fold2[:, :, 16:32], ALU.add).then_inc(fold_step, 1)

            def step(t):
                g1, g2, nxt = t.back(1), t.back(2), t.back(-1)
                if t.exists():
                    side_values_lo(0, 0, t)
                if g1.exists():
                    rstd_of(3, g1, res_step, 5, 4)
                if t.exists():
                    side_values_lo(0, 1, t)
                    sides_lo_of(0, t)
                    self_bias(0, t)
                if nxt.exists():
                    rstd_of(0, nxt, ln0_step, 4, 3)
                if t.exists():
                    rstd_of(1, t, ctx_step[0], 7, 4)
                if g2.exists():
                    fold_again(g2)
                    fold_last(g2)
                if g1.exists():
                    scale_adj(g1)
                if g2.exists():
                    v_lo_of(g2)
                    probs_lo(0, g2)
                    probs_lo(1, g2)
                    probs_lo(2, g2)
                if g1.exists():
                    residual_and_bias(g1)
                if t.exists():
                    side_values_lo(1, 0, t)
                    side_values_lo(1, 1, t)
                    sides_lo_of(1, t)
                    self_bias(1, t)
                    rstd_of(2, t, ctx_step[1], 7, 4)
                if g2.exists():
                    output(g2)
                if g1.exists():
                    fold_scores(g1)

            rstd_of(0, Graph(0, 0, B - 1), ln0_step, 4, 3)
            pool.wait_ge(bounds_made, n_weights)
            pool.partition_all_reduce(bound_all[:, :], bounds[:, :], 128,
                                      bass.bass_isa.ReduceOp.max).then_inc(bounds_shared, 1)
            pool.wait_ge(prepared, 1)
            run_pipeline(pool, step)

        @block.scalar
        def _(act):
            load_small(act, 1)
            def split_high(n):
                act.activation(weight(wd_hi, wm_hi, n), weight(wd_raw, wm_raw, n), ACT.Copy,
                               scale=scale_of(n)).then_inc(w_split_hi, 1)

            def hT_hi_of(s, g, last_read):
                act.wait_ge(tr_done[s], g.at(1, 1))
                if g.back(1).begun():
                    act.wait_ge(last_read, g.back(1).at(1, 1))
                act.activation(hT_hi[s][:, :, :], t_ps[s].rearrange("p (c n) -> p c n", c=C), ACT.Relu).then_inc(hT_hi_made[s], 1)

            def graph_exp(l, g):
                act.wait_ge(soft_step[l], g.at(10, 2))
                act.activation(e_u[l][:, :], u_ps[l], ACT.Exp, bias=row[l][:, 1:2],
                               scale=SCALE / H_SCALE ** 2 if l == 0 else u_scale1,
                               accum_out=row[l][:, 2:3]).then_inc(exp_done[l], 1)

            def side_values_hi(l, side, g):
                act.wait_ge(val_made[l], g.at(2, side + 1))
                if g.back(1).begun():
                    act.wait_ge(ctx_done[l], g.back(1).at(1, 1))
                if g.back(1).begun():
                    act.wait_ge(val_lo_made[l], g.back(1).at(2, side + 1))
                act.activation(val_hi[l][:, side, :], val[l][:, side, :], ACT.Copy).then_inc(val_hi_made[l], 1)

            def sides_hi_of(l, g):
                act.wait_ge(sides_made[l], g.at(1, 1))
                if g.back(1).begun():
                    act.wait_ge(ctx_done[l], g.back(1).at(1, 1))
                if g.back(1).begun():
                    act.wait_ge(sides_lo_made[l], g.back(1).at(1, 1))
                act.activation(sides_hi[l][:, :, :], sides[l][:, :, :], ACT.Copy).then_inc(sides_hi_made[l], 1)

            def head_exps(r, g):
                act.wait_ge(score_made, g.at(R, r + 1))
                if r == 0:
                    if g.back(1).begun():
                        act.wait_ge(pT_done, g.back(1).at(C, C))
                for c in range(C):
                    ins = act.activation(prob[:, r, c, :], score_neg[:, r, c, :], ACT.Exp, bias=top_neg[:, r, c:c + 1],
                                         scale=-1.0)
                ins.then_inc(prob_made, 1)

            def self_copy(l, g):
                act.wait_ge(val_done[l][SELF], g.at(1, 1))
                if g.back(1).begun():
                    act.wait_ge(self_made[l], g.back(1).at(1, 1))
                act.activation(self_raw[l][:, :], val_ps[l][SELF][:, 0:D], ACT.Copy,
                               scale=VAL_SCALE * P_SCALE).then_inc(self_copied[l], 1)

            def qk_hi(n, g):
                ps, dst, s = ((q_ps, q_hi, SCALE * 2.0 ** -15), (k_ps, k_hi, VAL_SCALE))[n]
                act.wait_ge(qk_done, g.at(2, n + 1))
                if g.back(1).begun():
                    act.wait_ge(s_done, g.back(1).at(R, R))
                act.activation(dst[:, :, :], ps[:, 0:D].rearrange("p (c n) -> p c n", c=C), ACT.Copy,
                               scale=s).then_inc(qk_hi_made, 1)

            def probs_hi(b, g):
                act.wait_ge(pT_done, g.at(C, b + 1))
                if g.back(1).begun():
                    act.wait_ge(pv_done, g.back(1).at(1, 1))
                    act.wait_ge(pT_lo_made, g.back(1).at(C, b + 1))
                act.activation(pT_hi[:, b], pT_ps[b][:, :].rearrange("p (a n) -> p a n", a=R), ACT.Copy,
                               scale=P_SCALE).then_inc(pT_hi_made, 1)
                act.activation(pT[:, b, :], pT_ps[b][:, :], ACT.Copy, scale=P_SCALE).then_inc(pT_copied, 1)

            def oT_hi_of(g):
                act.wait_ge(oT_done, g.at(1, 1))
                if g.back(1).begun():
                    act.wait_ge(wo_done, g.back(1).at(1, 1))
                act.activation(oT_hi[:, :, :], oT_ps.rearrange("p (c n) -> p c n", c=C), ACT.Copy).then_inc(oT_hi_made, 1)

            def scale_output(g):
                act.wait_ge(wo_done, g.at(1, 1))
                if g.back(1).begun():
                    act.wait_ge(out_made, g.back(1).at(1, 1))
                act.activation(out_raw[:, :], wo_ps, ACT.Identity, scale=out_scale).then_inc(out_scaled, 1)

            def v_hi_of(g):
                act.wait_ge(v_made, g.at(1, 1))
                if g.back(1).begun():
                    act.wait_ge(pv_done, g.back(1).at(1, 1))
                    act.wait_ge(v_lo_made, g.back(1).at(1, 1))
                act.activation(v_hi[:, :, 0:HD], v_sb[:, :].rearrange("p (h d) -> p h d", h=H), ACT.Copy).then_inc(v_hi_made, 1)

            def step(t):
                g1, g2, nxt = t.back(1), t.back(2), t.back(-1)
                if g2.exists():
                    head_exps(3, g2)
                if t.exists():
                    graph_exp(0, t)
                    if t.first():
                        split_high(3)
                        split_high(4)
                        split_high(5)
                    side_values_hi(0, 0, t)
                    side_values_hi(0, 1, t)
                    sides_hi_of(0, t)
                    self_copy(0, t)
                if g1.exists():
                    hT_hi_of(2, g1, v_done)
                    qk_hi(0, g1)
                if g2.exists():
                    probs_hi(0, g2)
                if g1.exists():
                    qk_hi(1, g1)
                if g2.exists():
                    v_hi_of(g2)
                if t.exists():
                    hT_hi_of(1, t, val_done[1][SELF])
                    if t.first():
                        split_high(6)
                        split_high(7)
                        split_high(8)
                        split_high(9)
                if g2.exists():
                    probs_hi(1, g2)
                    probs_hi(2, g2)
                if t.exists():
                    graph_exp(1, t)
                if nxt.exists():
                    hT_hi_of(0, nxt, val_done[0][SELF])
                if t.exists():
                    side_values_hi(1, 0, t)
                    side_values_hi(1, 1, t)
                    sides_hi_of(1, t)
                if g1.exists():
                    head_exps(0, g1)
                if t.exists():
                    self_copy(1, t)
                if g2.exists():
                    oT_hi_of(g2)
                if g1.exists():
                    head_exps(1, g1)
                    head_exps(2, g1)
                if g2.exists():
                    scale_output(g2)

            hT_hi_of(0, Graph(0, 0, B - 1), u_done[0])
            act.wait_ge(scales_made, 1)
            for n in range(3):
                split_high(n)
            act.wait_ge(prepared, 1)
            run_pipeline(act, step)

        @block.vector
        def _(dve):
            steps = [0]

            def own(ins):
                steps[0] += 1
                ins.then_inc(scale_step, 1)
                dve.wait_ge(scale_step, steps[0])

            def absmax(dst, src):
                return dve.tensor_reduce(dst, src, X_AXIS, ALU.max, apply_absolute_value=True)

            def inverse_power_of_two(dst, power, src):
                own(dve.tensor_scalar(power.bitcast(I32), src.bitcast(I32), EXPONENT_BITS, None, ALU.bitwise_and))
                own(dve.reciprocal(dst, power))

            def split_low(n):
                dve.wait_ge(w_split_hi, n + 1)
                dve.scalar_tensor_tensor(weight(wd_lo, wm_lo, n), weight(wd_raw, wm_raw, n), scale_of(n),
                                         weight(wd_hi, wm_hi, n), ALU.mult, ALU.subtract).then_inc(w_split_lo, 1)

            def sums_of(src, s, sm):
                dve.bn_stats(stats[s][:, :], src).then_inc(sm, 1)

            def mean_var_of(s, sm, per, k, g):
                dve.wait_ge(sm, g.at(per, k))
                apart(dve, s)
                dve.bn_aggr(mean_var[s][:, :], stats[s][:, :]).then_inc(sm, 1)

            def outer_var(s, sm, per, k, g):
                dve.wait_ge(sm, g.at(per, k))
                dve.tensor_scalar(var2[s][:, :], mean_var[s][:, 1:2], LN_EPS, H_SCALE ** -2, ALU.add,
                                  ALU.mult).then_inc(sm, 1)

            def normalise(src, s, h, sm, g):
                dve.wait_ge(rstd_made[s], g.at(1, 1))
                if g.back(1).begun():
                    dve.wait_ge(tr_done[h], g.back(1).at(1, 1))
                dve.tensor_scalar(h_nat[h][:, :], src, mean_var[s][:, 0:1], rstd[s][:, :], ALU.subtract,
                                  ALU.mult).then_inc(sm, 1)

            def input_sums(g):
                dve.wait_ge(x_loaded[g.parity], g.loads())
                sums_of(x_in[:, g.parity, :], 0, ln0_step)

            def hT_lo_of(s, g):
                dve.wait_ge(hT_hi_made[s], g.at(1, 1))
                dve.scalar_tensor_tensor(hT_lo[s][:, :, :], t_ps[s].rearrange("p (c n) -> p c n", c=C), 0.0,
                                         hT_hi[s][:, :, :], ALU.max, ALU.subtract).then_inc(hT_lo_made[s], 1)

            def soft_max(l, g):
                dve.wait_ge(u_done[l], g.at(1, 1))
                dve.tensor_reduce(row[l][:, 0:1], u_ps[l], X_AXIS, ALU.max, negate=True).then_inc(soft_step[l], 1)

            def soft_max_scaled(l, g):
                dve.wait_ge(soft_step[l], g.at(10, 1))
                dve.tensor_scalar(row[l][:, 1:2], row[l][:, 0:1], SCALE / H_SCALE ** 2 if l == 0 else u_scale1, None,
                                  ALU.mult).then_inc(soft_step[l], 1)

            def soft_masked(l, g):
                dve.wait_ge(exp_done[l], g.at(1, 1))
                if l == 0:
                    dve.wait_ge(adj_loaded[g.parity], g.loads())
                dve.tensor_tensor_reduce(masked[l][:, :], e_u[l][:, :], adj_in[:, g.parity, :], 1.0, 0.0,
                                         ALU.mult, ALU.add, row[l][:, 4:5]).then_inc(soft_step[l], 1)

            def soft_sums(l, g):
                dve.wait_ge(soft_step[l], g.at(10, 3))
                dve.scalar_tensor_tensor(row[l][:, 5:6], row[l][:, 4:5], 0.0, row[l][:, 4:5], ALU.is_equal,
                                         ALU.add).then_inc(soft_step[l], 1)
                dve.scalar_tensor_tensor(row[l][:, 6:7], row[l][:, 2:3], SUM_EPS, row[l][:, 4:5], ALU.mult,
                                         ALU.add).then_inc(soft_step[l], 1)

            def soft_inverses(l, g):
                dve.wait_ge(soft_step[l], g.at(10, 5))
                dve.reciprocal(row[l][:, 7:9], row[l][:, 5:7]).then_inc(soft_step[l], 1)

            def soft_attn(l, g):
                dve.wait_ge(soft_step[l], g.at(10, 6))
                if g.back(1).begun():
                    dve.wait_ge(attnT_done[l], g.back(1).at(1, 1))
                dve.tensor_scalar(attn[l][:, :], masked[l][:, :], row[l][:, 7:8], P_SCALE, ALU.mult,
                                  ALU.mult).then_inc(soft_step[l], 1)

            def soft_diagonal(l, g):
                dve.tensor_tensor_reduce(diag_junk[l][:, :], masked[l][:, :], ident[:, :], 1.0, 0.0,
                                         ALU.mult, ALU.add, row[l][:, 3:4]).then_inc(soft_step[l], 1)

            def soft_factors(l, g):
                dve.wait_ge(soft_step[l], g.at(10, 8))
                dve.tensor_tensor(row[l][:, 9:11], row[l][:, 3:5], row[l][:, 7:9], ALU.mult).then_inc(soft_step[l], 1)

            def soft_factor_squared(l, g):
                dve.wait_ge(soft_step[l], g.at(10, 9))
                dve.tensor_tensor(row[l][:, 11:12], row[l][:, 10:11], row[l][:, 10:11], ALU.mult).then_inc(soft_step[l], 1)

            def side_values(l, side, g):
                w = (LEFT, RIGHT)[side]
                dve.wait_ge(val_done[l][w], g.at(1, 1))
                if g.back(1).begun():
                    dve.wait_ge(val_lo_made[l], g.back(1).at(2, side + 1))
                dve.scalar_tensor_tensor(val[l][:, side, :], val_ps[l][w][:, 0:D], VAL_SCALE, bd[:, l, w, :],
                                         ALU.mult, ALU.add).then_inc(val_made[l], 1)

            def attn_sides(l, g):
                dve.wait_ge(attnT_done[l], g.at(1, 1))
                if g.back(1).begun():
                    dve.wait_ge(sides_hi_made[l], g.back(1).at(1, 1))
                    dve.wait_ge(sides_lo_made[l], g.back(1).at(1, 1))
                dve.tensor_tensor(sides[l][:, :, :], attnT_ps[l].unsqueeze(1).broadcast_to([128, 2, 128]),
                                  side_mask[:, :, :], ALU.mult).then_inc(sides_made[l], 1)

            def digcn_ctx(l, g):
                dve.wait_ge(soft_step[l], g.at(10, 9))
                dve.wait_ge(self_made[l], g.at(1, 1))
                dve.wait_ge(ctx_done[l], g.at(1, 1))
                dve.scalar_tensor_tensor(ctx_sb[l][:, :], self_val[l][:, :], row[l][:, 9:10], ctx_ps[l][:, 0:D],
                                         ALU.mult, ALU.add).then_inc(ctx_step[l], 1)

            def digcn_sums(l, g):
                dve.wait_ge(ctx_step[l], g.at(7, 1))
                sums_of(ctx_sb[l][:, :], 1 + l, ctx_step[l])

            def digcn_var(l, g):
                dve.wait_ge(ctx_step[l], g.at(7, 3))
                dve.wait_ge(soft_step[l], g.at(10, 10))
                dve.tensor_scalar(var2[1 + l][:, :], mean_var[1 + l][:, 1:2], row[l][:, 11:12], eps_l[l],
                                  ALU.mult, ALU.add).then_inc(ctx_step[l], 1)

            def digcn_centre(l, g):
                dve.scalar_tensor_tensor(ln_t[l][:, :], ctx_sb[l][:, :], mean_var[1 + l][:, 0:1], lnw[:, l, :],
                                         ALU.subtract, ALU.mult).then_inc(ctx_step[l], 1)

            def digcn_factor(l, g):
                dve.wait_ge(rstd_made[1 + l], g.at(1, 1))
                dve.wait_ge(soft_step[l], g.at(10, 9))
                dve.tensor_tensor(row[l][:, 12:13], rstd[1 + l][:, :], row[l][:, 10:11], ALU.mult).then_inc(ctx_step[l], 1)

            def digcn_norm(l, g):
                dve.wait_ge(ctx_step[l], g.at(7, 6))
                if l == 0:
                    if g.back(1).begun():
                        dve.wait_ge(tr_done[1], g.back(1).at(1, 1))
                dst = h_nat[1] if l == 0 else ln_out
                dve.scalar_tensor_tensor(dst[:, :], ln_t[l][:, :], row[l][:, 12:13], lnb[:, l, :], ALU.mult,
                                         ALU.add).then_inc(ctx_step[l], 1)

            def residual(g):
                dve.wait_ge(ctx_step[1], g.at(7, 7))
                if g.back(1).begun():
                    dve.wait_ge(x1_bo_made, g.back(1).at(1, 1))
                dve.scalar_tensor_tensor(x1[:, :], ln_out[:, :], 0.0, x_in[:, g.parity, :], ALU.max,
                                         ALU.add).then_inc(res_step, 1)

            def residual_sums(g):
                dve.wait_ge(res_step, g.at(5, 1))
                sums_of(x1[:, :], 3, res_step)

            def qk_lo(n, g):
                ps, hi, lo, s = ((q_ps, q_hi, q_lo, SCALE * 2.0 ** -15), (k_ps, k_hi, k_lo, VAL_SCALE))[n]
                dve.wait_ge(qk_hi_made, g.at(2, n + 1))
                dve.scalar_tensor_tensor(lo[:, :, :], ps[:, 0:D].rearrange("p (c n) -> p c n", c=C), s, hi[:, :, :],
                                         ALU.mult, ALU.subtract).then_inc(qk_lo_made, 1)

            def v_biased(g):
                dve.wait_ge(v_done, g.at(1, 1))
                if g.back(1).begun():
                    dve.wait_ge(v_lo_made, g.back(1).at(1, 1))
                dve.scalar_tensor_tensor(v_sb[:, :], v_ps[:, 0:D], VAL_SCALE, bv_b[:, :], ALU.mult,
                                         ALU.add).then_inc(v_made, 1)

            def head_scores(r, g):
                dve.wait_ge(s_done, g.at(R, r + 1))
                if r == 0:
                    dve.wait_ge(adj_scaled, g.at(1, 1))
                    if g.back(1).begun():
                        dve.wait_ge(fold_step, g.back(1).at(3, 1))
                        dve.wait_ge(prob_made, g.back(1).at(R, R))
                        dve.wait_ge(pad_step, g.back(1).at(3, 2))
                apart(dve, 4 + r)
                for c in range(C):
                    ins = dve.tensor_tensor_reduce(score_neg[:, r, c, :], s_ps[r][:, c * 128:(c + 1) * 128], adj_s[:, :],
                                                   s_scale_neg, HIGHEST, ALU.add, ALU.min, top_neg[:, r, c:c + 1])
                ins.then_inc(score_made, 1)

            flat = "p r c -> p (r c)"

            def pad_sums(g):
                dve.wait_ge(fold_step, g.at(3, 3))
                dve.tensor_reduce(score_sum[:, :], fold3[:, :, :], X_AXIS, ALU.add).then_inc(pad_step, 1)
                dve.tensor_scalar(top_nonzero[:, :], top_neg[:, :, :].rearrange(flat), 0.0, None,
                                  ALU.not_equal).then_inc(pad_step, 1)

            def pad_kept(g):
                dve.wait_ge(pad_step, g.at(3, 2))
                dve.scalar_tensor_tensor(kept[:, :, :].rearrange(flat), score_sum[:, :], 0.0, top_nonzero[:, :],
                                         ALU.not_equal, ALU.max).then_inc(pad_step, 1)

            pv = pv_ps.rearrange("p (h d) -> p h d", h=H)

            def inverse_sums(g):
                dve.wait_ge(pv_done, g.at(1, 1))
                dve.reciprocal(inv_sum[:, :].unsqueeze(2), pv[:, :, HD:HD + 1]).then_inc(o_step, 1)

            def inverse_kept(g):
                dve.wait_ge(o_step, g.at(3, 1))
                dve.wait_ge(pad_step, g.at(3, 3))
                dve.tensor_tensor(inv_kept[:, :].rearrange("p (c r) -> p c r", c=C),
                                  inv_sum[:, :].rearrange("p (c r) -> p c r", c=C),
                                  kept[:, :, :].rearrange("p r c -> p c r"), ALU.mult).then_inc(o_step, 1)

            def head_outputs(g):
                dve.wait_ge(o_step, g.at(3, 2))
                if g.back(1).begun():
                    dve.wait_ge(oT_done, g.back(1).at(1, 1))
                dve.tensor_tensor(o_nat[:, :].rearrange("p (h d) -> p h d", h=H), pv[:, :, 0:HD],
                                  inv_kept[:, :].unsqueeze(2).broadcast_to([128, H, HD]), ALU.mult).then_inc(o_step, 1)

            def oT_lo_of(g):
                dve.wait_ge(oT_hi_made, g.at(1, 1))
                dve.tensor_tensor(oT_lo[:, :, :], oT_ps.rearrange("p (c n) -> p c n", c=C), oT_hi[:, :, :],
                                  ALU.subtract).then_inc(oT_lo_made, 1)

            def step(t):
                g1, g2, nxt = t.back(1), t.back(2), t.back(-1)
                if t.exists():
                    soft_max(0, t)
                if g1.exists():
                    digcn_centre(1, g1)
                if t.exists():
                    soft_max_scaled(0, t)
                if g1.exists():
                    digcn_factor(1, g1)
                    digcn_norm(1, g1)
                if t.exists():
                    soft_masked(0, t)
                if g1.exists():
                    residual(g1)
                if t.exists():
                    soft_sums(0, t)
                    side_values(0, 0, t)
                    soft_inverses(0, t)
                if g1.exists():
                    residual_sums(g1)
                if t.exists():
                    soft_attn(0, t)
                    if t.first():
                        split_low(3)
                if g1.exists():
                    mean_var_of(3, res_step, 5, 2, g1)
                if t.exists():
                    side_values(0, 1, t)
                    if t.first():
                        split_low(5)
                if g1.exists():
                    outer_var(3, res_step, 5, 3, g1)
                if t.exists():
                    attn_sides(0, t)
                    if t.first():
                        split_low(4)
                    soft_diagonal(0, t)
                if g1.exists():
                    normalise(x1[:, :], 3, 2, res_step, g1)
                if g2.exists():
                    v_biased(g2)
                if t.exists():
                    soft_factors(0, t)
                if nxt.exists():
                    input_sums(nxt)
                    mean_var_of(0, ln0_step, 4, 1, nxt)
                if g1.exists():
                    hT_lo_of(2, g1)
                if nxt.exists():
                    outer_var(0, ln0_step, 4, 2, nxt)
                if t.exists():
                    digcn_ctx(0, t)
                    soft_factor_squared(0, t)
                    digcn_sums(0, t)
                    mean_var_of(1, ctx_step[0], 7, 2, t)
                    digcn_var(0, t)
                    digcn_centre(0, t)
                if nxt.exists():
                    normalise(x_in[:, nxt.parity, :], 0, 0, ln0_step, nxt)
                if t.exists():
                    digcn_factor(0, t)
                    digcn_norm(0, t)
                if g1.exists():
                    qk_lo(0, g1)
                    qk_lo(1, g1)
                if g2.exists():
                    pad_sums(g2)
                if t.exists():
                    hT_lo_of(1, t)
                    if t.first():
                        split_low(6)
                if g1.exists():
                    head_scores(0, g1)
                    head_scores(1, g1)
                if t.exists():
                    soft_max(1, t)
                    if t.first():
                        split_low(7)
                    soft_max_scaled(1, t)
                    side_values(1, 0, t)
                    soft_masked(1, t)
                    soft_sums(1, t)
                    soft_inverses(1, t)
                    soft_attn(1, t)
                    if t.first():
                        split_low(8)
                    side_values(1, 1, t)
                    attn_sides(1, t)
                    if t.first():
                        split_low(9)
                if g2.exists():
                    pad_kept(g2)
                    inverse_sums(g2)
                    inverse_kept(g2)
                if t.exists():
                    soft_diagonal(1, t)
                if g2.exists():
                    head_outputs(g2)
                if nxt.exists():
                    hT_lo_of(0, nxt)
                if t.exists():
                    soft_factors(1, t)
                if g1.exists():
                    head_scores(2, g1)
                if g2.exists():
                    oT_lo_of(g2)
                if t.exists():
                    soft_factor_squared(1, t)
                    digcn_ctx(1, t)
                if g1.exists():
                    head_scores(3, g1)
                if t.exists():
                    digcn_sums(1, t)
                    mean_var_of(2, ctx_step[1], 7, 2, t)
                    digcn_var(1, t)

            g0 = Graph(0, 0, B - 1)
            input_sums(g0)
            mean_var_of(0, ln0_step, 4, 1, g0)
            outer_var(0, ln0_step, 4, 2, g0)
            normalise(x_in[:, 0, :], 0, 0, ln0_step, g0)
            dve.wait_ge(consts_made, 9)
            dve.wait_ge(small_in, 16 * n_small)
            for l in range(L):
                absmax(bias_max[:, l:l + 1], bd[:, l].rearrange("p w e -> p (w e)"))
            absmax(bias_max[:, 2:3], bv_b[:, :])
            absmax(bias_max[:, 3:4], lnw[:, 0, :])
            own(absmax(bias_max[:, 4:5], lnb[:, 0, :]))
            own(dve.tensor_tensor(h_need[:, :], bias_max[:, 3:4], bias_max[:, 4:5], ALU.add))
            own(dve.tensor_scalar(h_need[:, :], h_need[:, :], SMALLEST, None, ALU.max))
            inverse_power_of_two(tmp_a, tmp_b, h_need[:, :])
            own(dve.tensor_scalar(s_h1, tmp_a, H_SCALE / 2, None, ALU.mult))
            own(dve.tensor_scalar(ratio1, s_h1, 1.0 / (H_SCALE * D), None, ALU.mult))
            dve.tensor_scalar(least[:, 0:1], bias_max[:, 0:1], 1.0 / D, SMALLEST, ALU.mult, ALU.max)
            own(dve.tensor_tensor(tmp_a, bias_max[:, 1:2], ratio1, ALU.mult))
            dve.tensor_scalar(least[:, 1:2], tmp_a, SMALLEST, None, ALU.max)
            own(dve.tensor_scalar(least[:, 4:5], bias_max[:, 2:3], 1.0 / D, SMALLEST, ALU.mult, ALU.max))
            dve.tensor_scalar(lnw[:, 0, :], lnw[:, 0, :], s_h1, None, ALU.mult)
            dve.tensor_scalar(lnb[:, 0, :], lnb[:, 0, :], s_h1, None, ALU.mult)
            own(dve.tensor_tensor(tmp_a, s_h1, s_h1, ALU.mult))
            own(dve.reciprocal(tmp_b, tmp_a))
            own(dve.tensor_scalar(u_scale1, tmp_b, SCALE, None, ALU.mult))
            hT_lo_of(0, g0)
            for n in range(n_weights):
                dve.wait_ge(weight_in[n], 16)
                absmax(bounds[:, n:n + 1], weight(wd_raw, wm_raw, n).rearrange("p c e -> p (c e)")).then_inc(bounds_made, 1)
            dve.wait_ge(bounds_shared, 1)
            dve.tensor_reduce(need[:, 0:L], bound_all[:, 0:3 * L].rearrange("p (l w) -> p l w", l=L), X_AXIS, ALU.max)
            own(dve.tensor_copy(need[:, L:L + 4], bound_all[:, 3 * L:n_weights]))
            own(dve.tensor_tensor(need[:, :], need[:, :], least[:, :], ALU.max))
            inverse_power_of_two(inv2[:, :], pow2[:, :], need[:, :])
            dve.tensor_scalar(scl[:, 0:L + 4], inv2[:, :], W_TOP, None, ALU.mult).then_inc(scales_made, 1)
            dve.wait_ge(scales_made, 1)
            dve.tensor_scalar(val0, s_w0, H_SCALE * VAL_SCALE, None, ALU.mult)
            dve.tensor_scalar(val_v, s_v, H_SCALE * VAL_SCALE, None, ALU.mult)
            own(dve.tensor_scalar(val1, s_w1, VAL_SCALE, None, ALU.mult))
            own(dve.tensor_tensor(val1, val1, s_h1, ALU.mult))
            for n in range(3):
                split_low(n)
            for l in range(L):
                dve.tensor_scalar(eps_l[l], val_scale[l], P_SCALE * DIGCN_EPS ** 0.5, None, ALU.mult)
            own(dve.tensor_scalar(tmp_a, s_q, 2.0 ** -14, None, ALU.mult))
            for l in range(L):
                dve.tensor_tensor(eps_l[l], eps_l[l], eps_l[l], ALU.mult)
            own(dve.tensor_tensor(adj_scale, tmp_a, s_k, ALU.mult))
            own(dve.tensor_tensor(tmp_b, val_v, s_o, ALU.mult))
            own(dve.tensor_scalar(tmp_a, adj_scale, -1.0, None, ALU.mult))
            dve.reciprocal(s_scale_neg, tmp_a)
            dve.reciprocal(out_scale, tmp_b)
            for l in range(L):
                for w in (LEFT, RIGHT):
                    dve.tensor_scalar(bd[:, l, w, :], bd[:, l, w, :], val_scale[l], None, ALU.mult)
                dve.tensor_scalar(bd[:, l, SELF, :], bd[:, l, SELF, :], val_scale[l], P_SCALE, ALU.mult, ALU.mult)
            dve.tensor_scalar(bv_b[:, :], bv_b[:, :], val_v, None, ALU.mult).then_inc(prepared, 1)
            dve.wait_ge(prepared, 1)
            run_pipeline(dve, step)

        @block.tensor
        def _(pe):
            def three(out_ap, a_hi, a_lo, b_hi, b_lo, first, last):
                pe.matmul(out_ap, a_hi, b_hi, start=first, stop=False)
                pe.matmul(out_ap, a_hi, b_lo, start=False, stop=False)
                return pe.matmul(out_ap, a_lo, b_hi, start=False, stop=last)

            def transposes(s, made, per, k, g):
                pe.wait_ge(made, g.at(per, k))
                for c in range(C):
                    ins = pe.transpose(t_ps[s][:, c * 128:(c + 1) * 128], h_nat[s][:, c * 128:(c + 1) * 128], ident[:, :])
                ins.then_inc(tr_done[s], 1)

            def graph_scores(l, g):
                for c in range(C):
                    hi, lo = hT_hi[l][:, c, :], hT_lo[l][:, c, :]
                    ins = three(u_ps[l], hi, lo, hi, lo, c == 0, c == C - 1)
                ins.then_inc(u_done[l], 1)

            def node_values(l, w, g):
                if g.first():
                    pe.wait_ge(w_split_lo, 3 * l + w + 1)
                for c in range(C):
                    ins = three(val_ps[l][w][:, 0:D], hT_hi[l][:, c, :], hT_lo[l][:, c, :], wd_hi[:, l, w, c, :],
                                wd_lo[:, l, w, c, :], c == 0, c == C - 1)
                ins.then_inc(val_done[l][w], 1)

            def transpose_attn(l, g):
                pe.wait_ge(soft_step[l], g.at(10, 7))
                pe.transpose(attnT_ps[l], attn[l][:, :], ident[:, :]).then_inc(attnT_done[l], 1)

            def weigh_values(l, g):
                pe.wait_ge(sides_lo_made[l], g.at(1, 1))
                for side in range(2):
                    pe.wait_ge(val_lo_made[l], g.at(2, side + 1))
                    ins = three(ctx_ps[l][:, 0:D], sides_hi[l][:, side, :], sides_lo[l][:, side, :],
                                val_hi[l][:, side, :], val_lo[l][:, side, :], side == 0, side == 1)
                ins.then_inc(ctx_done[l], 1)

            def project_qk(n, g):
                if g.first():
                    pe.wait_ge(w_split_lo, 3 * L + n + 1)
                pe.wait_ge(hT_lo_made[2], g.at(1, 1))
                ps = (q_ps, k_ps)[n]
                for e in range(C):
                    cols = slice(e * 128, (e + 1) * 128)
                    for c in range(C):
                        ins = three(ps[:, cols], wm_hi[:, n, c, cols], wm_lo[:, n, c, cols],
                                    hT_hi[2][:, c, :], hT_lo[2][:, c, :], c == 0, c == C - 1)
                ins.then_inc(qk_done, 1)

            def head_scores(r, g):
                if r == 0:
                    pe.wait_ge(qk_lo_made, g.at(2, 2))
                rows = slice(r * HD, (r + 1) * HD)
                for c in range(C):
                    ins = three(s_ps[r][:, c * 128:(c + 1) * 128], q_hi[rows, c, :], q_lo[rows, c, :],
                                k_hi[rows, c, :], k_lo[rows, c, :], True, True)
                ins.then_inc(s_done, 1)

            def transpose_probs(b, g):
                for a in range(R):
                    r, c = divmod(b * R + a, C)
                    if a == 0 or c == 0:
                        pe.wait_ge(prob_made, g.at(R, r + 1))
                    ins = pe.transpose(pT_ps[b][:, a * 128:(a + 1) * 128], prob[:, r, c, :], ident[:, :])
                ins.then_inc(pT_done, 1)

            def weigh_by_probs(g):
                pe.wait_ge(v_lo_made, g.at(1, 1))
                for b in range(C):
                    pe.wait_ge(pT_lo_made, g.at(C, b + 1))
                    for a in range(R):
                        r, c = divmod(b * R + a, C)
                        h = c * R + r
                        ins = three(pv_ps[:, h * (HD + 1):(h + 1) * (HD + 1)], pT_hi[:, b, a, :], pT_lo[:, b, a, :],
                                    v_hi[:, h, :], v_lo[:, h, :], True, True)
                ins.then_inc(pv_done, 1)

            def transpose_o(g):
                pe.wait_ge(o_step, g.at(3, 3))
                for c in range(C):
                    ins = pe.transpose(oT_ps[:, c * 128:(c + 1) * 128], o_nat[:, c * 128:(c + 1) * 128], ident[:, :])
                ins.then_inc(oT_done, 1)

            def project_v(g):
                if g.first():
                    pe.wait_ge(w_split_lo, 3 * L + WV + 1)
                for c in range(C):
                    ins = three(v_ps[:, 0:D], hT_hi[2][:, c, :], hT_lo[2][:, c, :], wm_hi[:, WV, c, :],
                                wm_lo[:, WV, c, :], c == 0, c == C - 1)
                ins.then_inc(v_done, 1)

            def project_out(g):
                if g.first():
                    pe.wait_ge(w_split_lo, 3 * L + WO + 1)
                pe.wait_ge(oT_lo_made, g.at(1, 1))
                for c in range(C):
                    ins = three(wo_ps, oT_hi[:, c, :], oT_lo[:, c, :], wm_hi[:, WO, c, :], wm_lo[:, WO, c, :],
                                c == 0, c == C - 1)
                ins.then_inc(wo_done, 1)

            def step(t):
                g1, g2, nxt = t.back(1), t.back(2), t.back(-1)
                if t.exists():
                    pe.wait_ge(hT_lo_made[0], t.at(1, 1))
                    pe.wait_ge(hT_lo_made[0], t.at(1, 1))
                    graph_scores(0, t)
                    if g1.exists():
                        pe.wait_ge(ctx_step[1], g1.at(7, 1))
                    node_values(0, LEFT, t)
                    if t.back(3).exists():
                        pe.wait_ge(out_scaled, t.back(3).at(1, 1))
                    elif g1.exists():
                        pe.wait_ge(self_copied[0], g1.at(1, 1))
                    node_values(0, RIGHT, t)
                if g2.exists():
                    if g1.exists():
                        pe.wait_ge(self_copied[1], g1.at(1, 1))
                    elif t.back(3).exists():
                        pe.wait_ge(v_made, t.back(3).at(1, 1))
                    project_v(g2)
                if t.exists():
                    if g2.exists():
                        pe.wait_ge(score_made, g2.at(R, 3))
                    elif g1.exists():
                        pe.wait_ge(sides_made[0], g1.at(1, 1))
                    transpose_attn(0, t)
                    pe.wait_ge(val_made[0], t.at(2, 2))
                    node_values(0, SELF, t)
                if g1.exists():
                    pe.wait_ge(val_made[1], g1.at(2, 2))
                    transposes(2, res_step, 5, 5, g1)
                if g2.exists():
                    if t.exists():
                        pe.wait_ge(val_made[0], t.at(2, 1))
                    elif g1.exists():
                        pe.wait_ge(ctx_step[1], g1.at(7, 1))
                    elif t.back(3).exists():
                        pe.wait_ge(pT_copied, t.back(3).at(C, 3))
                    transpose_probs(0, g2)
                if t.exists():
                    if g2.exists():
                        pe.wait_ge(score_made, g2.at(R, 4))
                    elif g1.exists():
                        pe.wait_ge(val_made[1], g1.at(2, 1))
                    weigh_values(0, t)
                if g1.exists():
                    pe.wait_ge(sides_made[1], g1.at(1, 1))
                    project_qk(0, g1)
                    if t.exists():
                        pe.wait_ge(ctx_step[0], t.at(7, 1))
                    elif g2.exists():
                        pe.wait_ge(score_made, g2.at(R, 4))
                    project_qk(1, g1)
                if nxt.exists():
                    pe.wait_ge(exp_done[0], t.at(1, 1))
                    transposes(0, ln0_step, 4, 4, nxt)
                if g2.exists():
                    if g1.exists():
                        pe.wait_ge(hT_lo_made[2], g1.at(1, 1))
                    elif t.back(3).exists():
                        pe.wait_ge(pT_copied, t.back(3).at(C, 2))
                    transpose_probs(1, g2)
                if t.exists():
                    if g2.exists():
                        pe.wait_ge(v_made, g2.at(1, 1))
                    elif g1.exists():
                        pe.wait_ge(self_copied[1], g1.at(1, 1))
                    transposes(1, ctx_step[0], 7, 7, t)
                if g2.exists():
                    pe.wait_ge(pT_copied, g2.at(C, 1))
                    transpose_probs(2, g2)
                if g1.exists():
                    pe.wait_ge(qk_lo_made, g1.at(2, 1))
                    head_scores(0, g1)
                    if t.exists():
                        pe.wait_ge(sides_made[0], t.at(1, 1))
                    elif g2.exists():
                        pe.wait_ge(score_made, g2.at(R, 3))
                    head_scores(1, g1)
                if t.exists():
                    pe.wait_ge(hT_lo_made[1], t.at(1, 1))
                    pe.wait_ge(hT_lo_made[1], t.at(1, 1))
                    graph_scores(1, t)
                    if g1.exists():
                        pe.wait_ge(qk_lo_made, g1.at(2, 2))
                    else:
                        pe.wait_ge(ctx_step[0], t.at(7, 1))
                    node_values(1, LEFT, t)
                    if g2.exists():
                        pe.wait_ge(pT_copied, g2.at(C, 2))
                    elif g1.exists():
                        pe.wait_ge(hT_lo_made[2], g1.at(1, 1))
                    node_values(1, RIGHT, t)
                if g2.exists():
                    if t.exists():
                        pe.wait_ge(val_made[1], t.at(2, 1))
                    elif g1.exists():
                        pe.wait_ge(qk_lo_made, g1.at(2, 2))
                    else:
                        pe.wait_ge(score_made, g2.at(R, 4))
                    weigh_by_probs(g2)
                if t.exists():
                    if g1.exists():
                        pe.wait_ge(score_made, g1.at(R, 1))
                    transpose_attn(1, t)
                    pe.wait_ge(exp_done[1], t.at(1, 1))
                    node_values(1, SELF, t)
                if g1.exists():
                    pe.wait_ge(score_made, g1.at(R, 2))
                    head_scores(2, g1)
                if g2.exists():
                    if t.exists():
                        pe.wait_ge(self_copied[0], t.at(1, 1))
                    elif t.back(3).exists():
                        pe.wait_ge(out_scaled, t.back(3).at(1, 1))
                    transpose_o(g2)
                if t.exists():
                    if g2.exists():
                        pe.wait_ge(pT_copied, g2.at(C, 3))
                    else:
                        pe.wait_ge(val_made[0], t.at(2, 1))
                    weigh_values(1, t)
                if g1.exists():
                    if g2.exists():
                        pe.wait_ge(o_step, g2.at(3, 3))
                    elif t.exists():
                        pe.wait_ge(val_made[1], t.at(2, 1))
                    head_scores(3, g1)
                if g2.exists():
                    pe.wait_ge(oT_lo_made, g2.at(1, 1))
                    project_out(g2)

            pe.wait_ge(consts_made, 9)
            transposes(0, ln0_step, 4, 4, Graph(0, 0, B - 1))
            run_pipeline(pe, step)


_OUT = ((128, 128, 384), "float32")


def kernel(**inputs):
    import numpy as _np
    import concourse.bacc as _bacc
    from concourse import mybir as _mybir
    from concourse.bass_utils import run_bass_kernel_spmd as _run

    a = {k: _np.asarray(v) for k, v in inputs.items()}
    arrays = {
        "x": a["x"],
        "adj": a["adj"],
        "w_digcn": _np.stack([a["L0_gnn_Wl"], a["L0_gnn_Ws"], a["L0_gnn_Wr"]], axis=1).transpose(0, 1, 3, 2),
        "b_digcn": _np.stack([a["L0_gnn_bl"], a["L0_gnn_bs"], a["L0_gnn_br"]], axis=1),
        "ln_w": a["L0_gnn_ln_w"],
        "ln_b": a["L0_gnn_ln_b"],
        "w_mha": _np.stack([a["L1_gnn_Wq"], a["L1_gnn_Wk"], a["L1_gnn_Wv"], a["L1_gnn_Wo"]]).transpose(0, 2, 1),
        "bv": a["L1_gnn_bv"],
        "bo": a["L1_gnn_bo"],
    }
    arrays = {f"in_{k}": _np.ascontiguousarray(v) for k, v in arrays.items()}
    nc = _bacc.Bacc("TRN2", target_bir_lowering=False, num_devices=1)
    args = [nc.dram_tensor(k, v.shape, _mybir.dt.from_np(v.dtype), kind="ExternalInput").ap() for k, v in arrays.items()]
    shape, dtype = _OUT
    res = nc.dram_tensor("out_0", shape, _mybir.dt.from_np(_np.dtype(dtype)), kind="ExternalOutput").ap()
    two_gnn_blocks(nc, *args, res)
    r = _run(nc, [arrays], core_ids=[0])
    return r.results[0]["out_0"]
```

```python
from contextlib import ExitStack

import concourse.bass as bass
from concourse import mybir

F32 = mybir.dt.float32
F16 = mybir.dt.float16
I32 = mybir.dt.int32
ALU = mybir.AluOpType
ACT = mybir.ActivationFunctionType
X_AXIS = mybir.AxisListType.X

LN_EPS = 1e-5
DIGCN_EPS = 1e-12
SUM_EPS = 1e-10

H_SCALE = 2.0 ** 10
P_SCALE = 2.0 ** 14
W_TOP = 2.0 ** 14
VAL_SCALE = 2.0 ** -19
SMALLEST = 2.0 ** -30
EXPONENT_BITS = 0x7F800000
HIGHEST = 3.0e38


class Graph:

    def __init__(self, pair, offset, last):
        self.base, self.offset, self.last = pair, offset, last
        self.pair, self.parity = pair + offset // 2, offset % 2

    def back(self, n):
        return Graph(self.base, self.offset - n, self.last)

    def in_loop(self):
        return not isinstance(self.base, int)

    def exists(self):
        return self.in_loop() or 0 <= 2 * self.base + self.offset <= self.last

    def first(self):
        return not self.in_loop() and 2 * self.base + self.offset == 0

    def begun(self):
        return self.in_loop() or 2 * self.base + self.offset >= 0

    def at(self, per, k):
        if self.in_loop():
            return self.base * (2 * per) + (per * self.offset + k)
        return per * min(2 * self.base + self.offset, self.last) + k

    def done(self):
        return self.at(1, 1)

    def loads(self):
        return self.base * 16 + (self.offset // 2 * 16 + 16)

    def earlier_loads(self):
        return self.base * 16 + self.offset // 2 * 16


def two_gnn_blocks(nc, x, adj, w_digcn, b_digcn, ln_w, ln_b, w_mha, bv, bo, out):
    B, S, D = x.shape
    L, W3 = w_digcn.shape[0], w_digcn.shape[1]
    C = D // 128
    H = 12
    HD = D // H
    R = 128 // HD
    SCALE = float(D) ** -0.5
    assert S == 128 and D == C * 128 and W3 == 3 and L == 2 and HD == 32 and B % 2 == 0
    LEFT, SELF, RIGHT = 0, 1, 2
    WV, WO = 2, 3

    with ExitStack() as ctx:
        def sb(name, shape, dt=F32):
            return ctx.enter_context(nc.sbuf_tensor(name, shape, dt))

        def sem(name):
            return ctx.enter_context(nc.semaphore(name))

        ident = sb("ident", [128, 128])
        side_mask = sb("side_mask", [128, 2, 128])
        wd_raw = sb("wd_raw", [128, L, 3, C, D])
        wm_raw = sb("wm_raw", [128, 4, C, D])
        wd_hi = sb("wd_hi", [128, L, 3, C, D], F16)
        wd_lo = sb("wd_lo", [128, L, 3, C, D], F16)
        wm_hi = sb("wm_hi", [128, 4, C, D], F16)
        wm_lo = sb("wm_lo", [128, 4, C, D], F16)
        bd = sb("bd", [128, L, 3, D])
        lnw = sb("lnw", [128, L, D])
        lnb = sb("lnb", [128, L, D])
        bv_b = sb("bv_b", [128, D])
        bo_b = sb("bo_b", [128, D])
        bounds = sb("bounds", [128, 3 * L + 4])
        bound_all = sb("bound_all", [128, 3 * L + 4])
        need = sb("need", [128, L + 4])
        least = sb("least", [128, L + 4])
        pow2 = sb("pow2", [128, L + 4])
        inv2 = sb("inv2", [128, L + 4])
        h_need = sb("h_need", [128, 1])
        spread = [b_digcn[l].rearrange("w e -> (w e)") for l in range(L)] + [bv, ln_w[0], ln_b[0]]
        spread_tiles = [sb(f"spread{n}", [128, src.shape[0] // 128]) for n, src in enumerate(spread)]
        bias_part = sb("bias_part", [128, len(spread)])
        bias_max = sb("bias_max", [128, len(spread)])
        scl = sb("scl", [128, 24])
        half_neg = sb("half_neg", [128, 1])
        col = iter(range(24))
        s_w0, s_w1, s_q, s_k, s_v, s_o, s_h1 = [scl[:, c:c + 1] for c in (next(col) for _ in range(7))]
        val0, val1, ratio1, u_scale1, eps0, eps1, val_v, adj_scale, s_scale_neg, out_scale, tmp_a, tmp_b = [
            scl[:, c:c + 1] for c in (next(col) for _ in range(12))]
        w_scale, val_scale, eps_l = (s_w0, s_w1), (val0, val1), (eps0, eps1)

        carrier = sb("carrier", [1, 8])

        x_in = sb("x_in", [128, 2, D])
        adj_in = sb("adj_in", [128, 2, 128])
        h_nat = [sb(f"h_nat{s}", [128, D]) for s in range(3)]
        hT_hi = [sb(f"hT_hi{s}", [128, C, 128], F16) for s in range(3)]
        hT_lo = [sb(f"hT_lo{s}", [128, C, 128], F16) for s in range(3)]
        stats = [sb(f"stats{s}", [128, 6]) for s in range(4)]
        mean_var = [sb(f"mean_var{s}", [128, 2]) for s in range(4)]
        var2 = [sb(f"var2_{s}", [128, 1]) for s in range(4)]
        rstd = [sb(f"rstd{s}", [128, 1]) for s in range(4)]
        row = [sb(f"row{l}", [128, 16]) for l in range(L)]
        e_u = [sb(f"e_u{l}", [128, 128]) for l in range(L)]
        masked = [sb(f"masked{l}", [128, 128]) for l in range(L)]
        diag_junk = [sb(f"diag_junk{l}", [128, 128]) for l in range(L)]
        attn = [sb(f"attn{l}", [128, 128]) for l in range(L)]
        sides = [sb(f"sides{l}", [128, 2, 128]) for l in range(L)]
        sides_hi = [sb(f"sides_hi{l}", [128, 2, 128], F16) for l in range(L)]
        sides_lo = [sb(f"sides_lo{l}", [128, 2, 128], F16) for l in range(L)]
        val = [sb(f"val{l}", [128, 2, D]) for l in range(L)]
        val_hi = [sb(f"val_hi{l}", [128, 2, D], F16) for l in range(L)]
        val_lo = [sb(f"val_lo{l}", [128, 2, D], F16) for l in range(L)]
        self_raw = [sb(f"self_raw{l}", [128, D]) for l in range(L)]
        self_val = [sb(f"self_val{l}", [128, D]) for l in range(L)]
        ctx_sb = [sb(f"ctx_sb{l}", [128, D]) for l in range(L)]
        ln_t = [sb(f"ln_t{l}", [128, D]) for l in range(L)]
        ln_out = sb("ln_out", [128, D])
        x1 = sb("x1", [128, D])
        x1_bo = sb("x1_bo", [128, 2, D])
        q_hi = sb("q_hi", [128, C, 128], F16)
        q_lo = sb("q_lo", [128, C, 128], F16)
        k_hi = sb("k_hi", [128, C, 128], F16)
        k_lo = sb("k_lo", [128, C, 128], F16)
        v_sb = sb("v_sb", [128, D])
        v_hi = sb("v_hi", [128, H, HD + 1], F16)
        v_lo = sb("v_lo", [128, H, HD + 1], F16)
        adj_s = sb("adj_s", [128, 128])
        score_neg = sb("score_neg", [128, R, C, 128])
        prob = sb("prob", [128, R, C, 128])
        top_neg = sb("top_neg", [128, R, C])
        score_junk = sb("score_junk", [128, R, C, 128])
        score_sum = sb("score_sum", [128, R, C])
        top_nonzero = sb("top_nonzero", [128, H])
        kept = sb("kept", [128, R, C])
        pT = sb("pT", [128, C, R * 128])
        pT_hi = sb("pT_hi", [128, C, R, 128], F16)
        pT_lo = sb("pT_lo", [128, C, R, 128], F16)
        inv_sum = sb("inv_sum", [128, H])
        inv_kept = sb("inv_kept", [128, H])
        o_nat = sb("o_nat", [128, D])
        oT_hi = sb("oT_hi", [128, C, 128], F16)
        oT_lo = sb("oT_lo", [128, C, 128], F16)
        out_raw = sb("out_raw", [128, D])
        out_sb = sb("out_sb", [128, 2, D])

        banks = [ctx.enter_context(nc.psum_tensor(f"bank{i}", [128, 512], F32)) for i in range(8)]
        u_ps = [banks[7][:, 0:128], banks[2][:, 0:128]]
        attnT_ps = [banks[1][:, 0:128], banks[4][:, 0:128]]
        val_ps = [(banks[6], banks[4], banks[0]), (banks[3], banks[4], banks[6])]
        ctx_ps = [banks[5], banks[5]]
        t_ps = [banks[3][:, 0:D], banks[5][:, 0:D], banks[3][:, 0:D]]
        q_ps, k_ps, v_ps = banks[7], banks[1], banks[0]
        s_ps = [banks[6], banks[0], banks[5], banks[0]]
        pT_ps = [banks[1], banks[4], banks[0]]
        pv_ps = banks[4][:, 0:H * (HD + 1)]
        oT_ps = banks[7][:, 0:D]
        wo_ps = banks[4][:, 0:D]

        n_weights = 3 * L + 4
        n_small = 5 * L + 2
        spread_in, bias_bounds_made, bias_bounds_shared = sem("spread_in"), sem("bias_bounds_made"), sem("bias_bounds_shared")
        weight_in, small_in = [sem(f"weight_in{n}") for n in range(n_weights)], sem("small_in")
        x_loaded = [sem("x_loaded0"), sem("x_loaded1")]
        adj_loaded = [sem("adj_loaded0"), sem("adj_loaded1")]
        out_stored = [sem("out_stored0"), sem("out_stored1")]
        consts_made, bounds_made, bounds_shared = sem("consts_made"), sem("bounds_made"), sem("bounds_shared")
        scale_step, scales_made, prepared = sem("scale_step"), sem("scales_made"), sem("prepared")
        w_split_hi, w_split_lo = sem("w_split_hi"), sem("w_split_lo")
        tr_done = [sem(f"tr_done{s}") for s in range(3)]
        u_done = [sem(f"u_done{l}") for l in range(L)]
        val_done = [[sem(f"val_done{l}{w}") for w in range(3)] for l in range(L)]
        attnT_done = [sem(f"attnT_done{l}") for l in range(L)]
        ctx_done = [sem(f"ctx_done{l}") for l in range(L)]
        qk_done, v_done = [sem("q_done"), sem("k_done")], sem("v_done")
        s_done = sem("s_done")
        pT_done = sem("pT_done")
        pv_done, oT_done, wo_done = sem("pv_done"), sem("oT_done"), sem("wo_done")
        ln0_step = [sem(f"ln0_step{k}") for k in range(4)]
        soft_step = [[sem(f"soft_step{l}_{k}") for k in range(10)] for l in range(L)]
        sides_made = [sem(f"sides_made{l}") for l in range(L)]
        val_made = [[sem(f"val_made{l}{side}") for side in range(2)] for l in range(L)]
        ctx_step = [[sem(f"ctx_step{l}_{k}") for k in range(7)] for l in range(L)]
        hT_lo_made = [sem(f"hT_lo_made{s}") for s in range(3)]
        res_step = [sem(f"res_step{k}") for k in range(5)]
        qk_lo_made, v_made = [sem("q_lo_made"), sem("k_lo_made")], sem("v_made")
        score_made = sem("score_made")
        pad_step = [sem(f"pad_step{k}") for k in range(2)]
        o_step = [sem(f"o_step{k}") for k in range(3)]
        oT_lo_made = sem("oT_lo_made")
        exp_done = [sem(f"exp_done{l}") for l in range(L)]
        sides_hi_made = [sem(f"sides_hi_made{l}") for l in range(L)]
        val_hi_made = [[sem(f"val_hi_made{l}{side}") for side in range(2)] for l in range(L)]
        hT_hi_made = [sem(f"hT_hi_made{s}") for s in range(3)]
        qk_hi_made, v_hi_made = [sem("q_hi_made"), sem("k_hi_made")], sem("v_hi_made")
        prob_made = sem("prob_made")
        score_summed = sem("score_summed")
        self_copied = [sem(f"self_copied{l}") for l in range(L)]
        pT_copied = sem("pT_copied")
        oT_hi_made, out_scaled = sem("oT_hi_made"), sem("out_scaled")
        rstd_made = [sem(f"rstd_made{s}") for s in range(4)]
        sides_lo_made = [sem(f"sides_lo_made{l}") for l in range(L)]
        val_lo_made = [[sem(f"val_lo_made{l}{side}") for side in range(2)] for l in range(L)]
        adj_scaled, v_lo_made = sem("adj_scaled"), sem("v_lo_made")
        x1_bo_made = sem("x1_bo_made")
        self_made = [sem(f"self_made{l}") for l in range(L)]
        pT_lo_made, out_made = sem("pT_lo_made"), sem("out_made")

        block = ctx.enter_context(nc.Block())

        def weight(wd, wm, n):
            return wd[:, n // 3, n % 3] if n < 3 * L else wm[:, n - 3 * L]

        def scale_of(n):
            return w_scale[n // 3] if n < 3 * L else (s_q, s_k, s_v, s_o)[n - 3 * L]

        def apart(eng, n):
            eng.memset(carrier[:, n:n + 1], 0.0)

        def run_pipeline(eng, step):
            first, last = 2, B // 2 - 1
            for pair in range(first):
                for parity in range(2):
                    step(Graph(pair, parity, B - 1))
            with eng.Fori(first, last) as pair:
                for parity in range(2):
                    step(Graph(pair, parity, B - 1))
            for pair in range(last, last + 2):
                for parity in range(2):
                    step(Graph(pair, parity, B - 1))

        @block.sync
        def _(sp):
            def load_x(g):
                i = 2 * g.pair + g.parity
                sp.dma_start(x_in[:, g.parity, :], x[bass.ds(i, 1), :, :].rearrange("a n d -> n (a d)")
                             ).then_inc(x_loaded[g.parity], 16)

            def load_adj(g):
                i = 2 * g.pair + g.parity
                sp.dma_start(adj_in[:, g.parity, :], adj[bass.ds(i, 1), :, :].rearrange("a n m -> n (a m)")
                             ).then_inc(adj_loaded[g.parity], 16)

            load_x(Graph(0, 0, B - 1))
            load_adj(Graph(0, 0, B - 1))
            for l in range(L):
                for w in range(3):
                    sp.dma_start(wd_raw[:, l, w, :, :],
                                 w_digcn[l, w].rearrange("(c p) e -> p c e", p=128)).then_inc(weight_in[3 * l + w], 16)
            for w in range(4):
                sp.dma_start(wm_raw[:, w, :, :],
                             w_mha[w].rearrange("(c p) e -> p c e", p=128)).then_inc(weight_in[3 * L + w], 16)

            small = [(bd[:, l, w, :], b_digcn[l, w]) for l in range(L) for w in range(3)]
            small += [(lnw[:, l, :], ln_w[l]) for l in range(L)] + [(lnb[:, l, :], ln_b[l]) for l in range(L)]
            for dst, src in small + [(bv_b[:, :], bv), (bo_b[:, :], bo)]:
                sp.dma_start(dst, src.partition_broadcast(128)).then_inc(small_in, 16)

            def step(t):
                g1, g2, nxt = t.back(1), t.back(2), t.back(-1)
                if nxt.exists():
                    if g1.begun():
                        sp.wait_ge(res_step[0], g1.done())
                    load_x(nxt)
                    if g1.begun():
                        sp.wait_ge(adj_scaled, g1.done())
                        sp.wait_ge(soft_step[1][2], g1.done())
                    load_adj(nxt)
                if g2.exists():
                    sp.wait_ge(out_made, g2.done())
                    i = 2 * g2.pair + g2.parity
                    sp.dma_start(out[bass.ds(i, 1), :, :].rearrange("a n d -> n (a d)"),
                                 out_sb[:, g2.parity, :]).then_inc(out_stored[g2.parity], 16)

            run_pipeline(sp, step)
            for p in range(2):
                sp.wait_ge(out_stored[p], 16 * (B // 2))

        @block.gpsimd
        def _(pool):
            pool.memset(ident[:, :], 0.0).then_inc(consts_made, 1)
            pool.memset(side_mask[:, :, :], 1.0).then_inc(consts_made, 1)
            pool.memset(v_hi[:, :, :], 1.0).then_inc(consts_made, 1)
            pool.memset(v_lo[:, :, :], 0.0).then_inc(consts_made, 1)
            pool.memset(half_neg[:, :], -0.5).then_inc(consts_made, 1)
            pool.memset(least[:, :], SMALLEST).then_inc(consts_made, 1)
            pool.wait_ge(consts_made, 6)
            pool.affine_select(out=ident[:, :], in_=ident[:, :], compare_op=ALU.not_equal, fill=1.0,
                               base=0, pattern=[[-1, 128]], channel_multiplier=1).then_inc(consts_made, 1)
            pool.affine_select(out=side_mask[:, 0, :], in_=side_mask[:, 0, :], compare_op=ALU.is_gt, fill=0.0,
                               base=0, pattern=[[-1, 128]], channel_multiplier=1).then_inc(consts_made, 1)
            pool.affine_select(out=side_mask[:, 1, :], in_=side_mask[:, 1, :], compare_op=ALU.is_gt, fill=0.0,
                               base=0, pattern=[[1, 128]], channel_multiplier=-1).then_inc(consts_made, 1)
            def rstd_of(s, g, var_made):
                pool.wait_ge(var_made, g.done())
                pool.tensor_tensor(rstd[s][:, :], var2[s][:, :], half_neg[:, :], ALU.pow).then_inc(rstd_made[s], 1)

            def side_values_lo(l, side, g):
                pool.wait_ge(val_hi_made[l][side], g.done())
                if g.back(1).begun():
                    pool.wait_ge(ctx_done[l], g.back(1).done())
                pool.tensor_tensor(val_lo[l][:, side, :], val[l][:, side, :], val_hi[l][:, side, :],
                                   ALU.subtract).then_inc(val_lo_made[l][side], 1)

            def sides_lo_of(l, g):
                pool.wait_ge(sides_hi_made[l], g.done())
                if g.back(1).begun():
                    pool.wait_ge(ctx_done[l], g.back(1).done())
                pool.tensor_tensor(sides_lo[l][:, :, :], sides[l][:, :, :], sides_hi[l][:, :, :],
                                   ALU.subtract).then_inc(sides_lo_made[l], 1)

            def self_bias(l, g):
                pool.wait_ge(self_copied[l], g.done())
                if g.back(1).begun():
                    pool.wait_ge(ctx_step[l][0], g.back(1).done())
                pool.tensor_tensor(self_val[l][:, :], self_raw[l][:, :], bd[:, l, SELF, :],
                                   ALU.add).then_inc(self_made[l], 1)

            def probs_lo(b, g):
                pool.wait_ge(pT_copied, g.at(C, b + 1))
                if g.back(1).begun():
                    pool.wait_ge(pv_done, g.back(1).done())
                pool.tensor_tensor(pT_lo[:, b].rearrange("p a n -> p (a n)"), pT[:, b, :],
                                   pT_hi[:, b].rearrange("p a n -> p (a n)"), ALU.subtract).then_inc(pT_lo_made, 1)

            def scale_adj(g):
                pool.wait_ge(adj_loaded[g.parity], g.loads())
                if g.back(1).begun():
                    pool.wait_ge(score_made, g.back(1).at(R, R))
                pool.tensor_tensor(adj_s[:, :], adj_in[:, g.parity, :], adj_scale.broadcast_to([128, 128]),
                                   ALU.mult).then_inc(adj_scaled, 1)

            def residual_and_bias(g):
                pool.wait_ge(res_step[0], g.done())
                if g.back(2).begun():
                    pool.wait_ge(out_made, g.back(2).done())
                pool.tensor_tensor(x1_bo[:, g.parity, :], x1[:, :], bo_b[:, :], ALU.add).then_inc(x1_bo_made, 1)

            def output(g):
                pool.wait_ge(out_scaled, g.done())
                if g.back(2).begun():
                    pool.wait_ge(out_stored[g.parity], g.earlier_loads())
                pool.tensor_tensor(out_sb[:, g.parity, :], out_raw[:, :], x1_bo[:, g.parity, :],
                                   ALU.add).then_inc(out_made, 1)

            def v_lo_of(g):
                pool.wait_ge(v_hi_made, g.done())
                if g.back(1).begun():
                    pool.wait_ge(pv_done, g.back(1).done())
                pool.tensor_tensor(v_lo[:, :, 0:HD], v_sb[:, :].rearrange("p (h d) -> p h d", h=H),
                                   v_hi[:, :, 0:HD], ALU.subtract).then_inc(v_lo_made, 1)

            def step(t):
                g1, g2, nxt = t.back(1), t.back(2), t.back(-1)
                if g1.exists():
                    scale_adj(g1)
                if g2.exists():
                    probs_lo(0, g2)
                if t.exists():
                    side_values_lo(0, 0, t)
                if g1.exists():
                    rstd_of(3, g1, res_step[3])
                if t.exists():
                    side_values_lo(0, 1, t)
                    sides_lo_of(0, t)
                    self_bias(0, t)
                if g2.exists():
                    v_lo_of(g2)
                    probs_lo(1, g2)
                if t.exists():
                    rstd_of(1, t, ctx_step[0][3])
                if g2.exists():
                    probs_lo(2, g2)
                if nxt.exists():
                    rstd_of(0, nxt, ln0_step[2])
                if g1.exists():
                    residual_and_bias(g1)
                if t.exists():
                    side_values_lo(1, 0, t)
                    side_values_lo(1, 1, t)
                    sides_lo_of(1, t)
                    self_bias(1, t)
                    rstd_of(2, t, ctx_step[1][3])
                if g2.exists():
                    output(g2)

            rstd_of(0, Graph(0, 0, B - 1), ln0_step[2])
            pool.wait_ge(bias_bounds_made, len(spread))
            pool.partition_all_reduce(bias_max[:, :], bias_part[:, :], 128,
                                      bass.bass_isa.ReduceOp.max).then_inc(bias_bounds_shared, 1)
            pool.wait_ge(bounds_made, n_weights)
            pool.partition_all_reduce(bound_all[:, :], bounds[:, :], 128,
                                      bass.bass_isa.ReduceOp.max).then_inc(bounds_shared, 1)
            pool.wait_ge(prepared, 1)
            run_pipeline(pool, step)

        @block.scalar
        def _(act):
            for tile, src in zip(spread_tiles, spread):
                act.dma_start(tile[:, :], src.rearrange("(p k) -> p k", p=128)).then_inc(spread_in, 16)
            def split_high(n):
                act.activation(weight(wd_hi, wm_hi, n), weight(wd_raw, wm_raw, n), ACT.Copy,
                               scale=scale_of(n)).then_inc(w_split_hi, 1)

            def hT_hi_of(s, g, last_read):
                act.wait_ge(tr_done[s], g.done())
                if g.back(1).begun():
                    act.wait_ge(last_read, g.back(1).done())
                act.activation(hT_hi[s][:, :, :], t_ps[s].rearrange("p (c n) -> p c n", c=C), ACT.Relu).then_inc(hT_hi_made[s], 1)

            def graph_exp(l, g):
                act.wait_ge(soft_step[l][1], g.done())
                act.activation(e_u[l][:, :], u_ps[l], ACT.Exp, bias=row[l][:, 1:2],
                               scale=SCALE / H_SCALE ** 2 if l == 0 else u_scale1,
                               accum_out=row[l][:, 2:3]).then_inc(exp_done[l], 1)

            def side_values_hi(l, side, g):
                act.wait_ge(val_made[l][side], g.done())
                if g.back(1).begun():
                    act.wait_ge(ctx_done[l], g.back(1).done())
                act.activation(val_hi[l][:, side, :], val[l][:, side, :], ACT.Copy).then_inc(val_hi_made[l][side], 1)

            def sides_hi_of(l, g):
                act.wait_ge(sides_made[l], g.done())
                if g.back(1).begun():
                    act.wait_ge(ctx_done[l], g.back(1).done())
                act.activation(sides_hi[l][:, :, :], sides[l][:, :, :], ACT.Copy).then_inc(sides_hi_made[l], 1)

            def head_exps(r, g):
                act.wait_ge(score_made, g.at(R, r + 1))
                if r == 0:
                    if g.back(1).begun():
                        act.wait_ge(pT_done, g.back(1).at(C, C))
                for c in range(C):
                    ins = act.activation(prob[:, r, c, :], score_neg[:, r, c, :], ACT.Exp, bias=top_neg[:, r, c:c + 1],
                                         scale=-1.0)
                ins.then_inc(prob_made, 1)

            def score_sums(r, g):
                act.wait_ge(score_made, g.at(R, r + 1))
                if r == 0:
                    if g.back(1).begun():
                        act.wait_ge(pad_step[1], g.back(1).done())
                for c in range(C):
                    ins = act.activation(score_junk[:, r, c, :], score_neg[:, r, c, :], ACT.Copy,
                                         accum_out=score_sum[:, r, c:c + 1])
                ins.then_inc(score_summed, 1)

            def self_copy(l, g):
                act.wait_ge(val_done[l][SELF], g.done())
                if g.back(1).begun():
                    act.wait_ge(self_made[l], g.back(1).done())
                act.activation(self_raw[l][:, :], val_ps[l][SELF][:, 0:D], ACT.Copy,
                               scale=VAL_SCALE * P_SCALE).then_inc(self_copied[l], 1)

            def qk_hi(n, g):
                ps, dst, s = ((q_ps, q_hi, SCALE * 2.0 ** -15), (k_ps, k_hi, VAL_SCALE))[n]
                act.wait_ge(qk_done[n], g.done())
                if g.back(1).begun():
                    act.wait_ge(s_done, g.back(1).at(R, R))
                act.activation(dst[:, :, :], ps[:, 0:D].rearrange("p (c n) -> p c n", c=C), ACT.Copy,
                               scale=s).then_inc(qk_hi_made[n], 1)

            def probs_hi(b, g):
                act.wait_ge(pT_done, g.at(C, b + 1))
                if g.back(1).begun():
                    act.wait_ge(pv_done, g.back(1).done())
                act.activation(pT_hi[:, b], pT_ps[b][:, :].rearrange("p (a n) -> p a n", a=R), ACT.Copy,
                               scale=P_SCALE)
                act.activation(pT[:, b, :], pT_ps[b][:, :], ACT.Copy, scale=P_SCALE).then_inc(pT_copied, 1)

            def oT_hi_of(g):
                act.wait_ge(oT_done, g.done())
                if g.back(1).begun():
                    act.wait_ge(wo_done, g.back(1).done())
                act.activation(oT_hi[:, :, :], oT_ps.rearrange("p (c n) -> p c n", c=C), ACT.Copy).then_inc(oT_hi_made, 1)

            def scale_output(g):
                act.wait_ge(wo_done, g.done())
                if g.back(1).begun():
                    act.wait_ge(out_made, g.back(1).done())
                act.activation(out_raw[:, :], wo_ps, ACT.Identity, scale=out_scale).then_inc(out_scaled, 1)

            def v_hi_of(g):
                act.wait_ge(v_made, g.done())
                if g.back(1).begun():
                    act.wait_ge(pv_done, g.back(1).done())
                act.activation(v_hi[:, :, 0:HD], v_sb[:, :].rearrange("p (h d) -> p h d", h=H), ACT.Copy).then_inc(v_hi_made, 1)

            def step(t):
                g1, g2, nxt = t.back(1), t.back(2), t.back(-1)
                if g2.exists():
                    head_exps(3, g2)
                if t.exists():
                    graph_exp(0, t)
                    if t.first():
                        split_high(3)
                        split_high(4)
                        split_high(5)
                if g2.exists():
                    probs_hi(0, g2)
                if t.exists():
                    side_values_hi(0, 0, t)
                if g2.exists():
                    score_sums(1, g2)
                if t.exists():
                    side_values_hi(0, 1, t)
                    self_copy(0, t)
                    sides_hi_of(0, t)
                if g2.exists():
                    score_sums(2, g2)
                if g1.exists():
                    hT_hi_of(2, g1, v_done)
                if g2.exists():
                    v_hi_of(g2)
                    probs_hi(1, g2)
                    probs_hi(2, g2)
                    score_sums(3, g2)
                if g1.exists():
                    qk_hi(0, g1)
                    qk_hi(1, g1)
                if t.exists():
                    hT_hi_of(1, t, val_done[1][SELF])
                    if t.first():
                        split_high(6)
                        split_high(7)
                        split_high(8)
                        split_high(9)
                    graph_exp(1, t)
                if g1.exists():
                    score_sums(0, g1)
                if t.exists():
                    side_values_hi(1, 0, t)
                    side_values_hi(1, 1, t)
                    sides_hi_of(1, t)
                if g2.exists():
                    oT_hi_of(g2)
                if nxt.exists():
                    hT_hi_of(0, nxt, val_done[0][SELF])
                if t.exists():
                    self_copy(1, t)
                if g1.exists():
                    head_exps(0, g1)
                    head_exps(1, g1)
                    head_exps(2, g1)
                if g2.exists():
                    scale_output(g2)

            hT_hi_of(0, Graph(0, 0, B - 1), u_done[0])
            act.wait_ge(scales_made, 1)
            for n in range(3):
                split_high(n)
            act.wait_ge(prepared, 1)
            run_pipeline(act, step)

        @block.vector
        def _(dve):
            steps = [0]

            def own(ins):
                steps[0] += 1
                ins.then_inc(scale_step, 1)
                dve.wait_ge(scale_step, steps[0])

            def absmax(dst, src):
                return dve.tensor_reduce(dst, src, X_AXIS, ALU.max, apply_absolute_value=True)

            def inverse_power_of_two(dst, power, src):
                own(dve.tensor_scalar(power.bitcast(I32), src.bitcast(I32), EXPONENT_BITS, None, ALU.bitwise_and))
                own(dve.reciprocal(dst, power))

            def split_low(n):
                dve.wait_ge(w_split_hi, n + 1)
                dve.scalar_tensor_tensor(weight(wd_lo, wm_lo, n), weight(wd_raw, wm_raw, n), scale_of(n),
                                         weight(wd_hi, wm_hi, n), ALU.mult, ALU.subtract).then_inc(w_split_lo, 1)

            def sums_of(src, s, sm):
                dve.bn_stats(stats[s][:, :], src).then_inc(sm, 1)

            def mean_var_of(s, sums_made, made, g):
                dve.wait_ge(sums_made, g.done())
                apart(dve, s)
                dve.bn_aggr(mean_var[s][:, :], stats[s][:, :]).then_inc(made, 1)

            def outer_var(s, mean_var_made, made, g):
                dve.wait_ge(mean_var_made, g.done())
                dve.tensor_scalar(var2[s][:, :], mean_var[s][:, 1:2], LN_EPS, H_SCALE ** -2, ALU.add,
                                  ALU.mult).then_inc(made, 1)

            def normalise(src, s, h, made, g):
                dve.wait_ge(rstd_made[s], g.done())
                if g.back(1).begun():
                    dve.wait_ge(tr_done[h], g.back(1).done())
                dve.tensor_scalar(h_nat[h][:, :], src, mean_var[s][:, 0:1], rstd[s][:, :], ALU.subtract,
                                  ALU.mult).then_inc(made, 1)

            def input_sums(g):
                dve.wait_ge(x_loaded[g.parity], g.loads())
                sums_of(x_in[:, g.parity, :], 0, ln0_step[0])

            def hT_lo_of(s, g):
                dve.wait_ge(hT_hi_made[s], g.done())
                dve.scalar_tensor_tensor(hT_lo[s][:, :, :], t_ps[s].rearrange("p (c n) -> p c n", c=C), 0.0,
                                         hT_hi[s][:, :, :], ALU.max, ALU.subtract).then_inc(hT_lo_made[s], 1)

            def soft_max(l, g):
                dve.wait_ge(u_done[l], g.done())
                dve.tensor_reduce(row[l][:, 0:1], u_ps[l], X_AXIS, ALU.max, negate=True).then_inc(soft_step[l][0], 1)

            def soft_max_scaled(l, g):
                dve.wait_ge(soft_step[l][0], g.done())
                dve.tensor_scalar(row[l][:, 1:2], row[l][:, 0:1], SCALE / H_SCALE ** 2 if l == 0 else u_scale1, None,
                                  ALU.mult).then_inc(soft_step[l][1], 1)

            def soft_masked(l, g):
                dve.wait_ge(exp_done[l], g.done())
                if l == 0:
                    dve.wait_ge(adj_loaded[g.parity], g.loads())
                dve.tensor_tensor_reduce(masked[l][:, :], e_u[l][:, :], adj_in[:, g.parity, :], 1.0, 0.0,
                                         ALU.mult, ALU.add, row[l][:, 4:5]).then_inc(soft_step[l][2], 1)

            def soft_sums(l, g):
                dve.wait_ge(soft_step[l][2], g.done())
                dve.scalar_tensor_tensor(row[l][:, 5:6], row[l][:, 4:5], 0.0, row[l][:, 4:5], ALU.is_equal,
                                         ALU.add).then_inc(soft_step[l][3], 1)
                dve.scalar_tensor_tensor(row[l][:, 6:7], row[l][:, 2:3], SUM_EPS, row[l][:, 4:5], ALU.mult,
                                         ALU.add).then_inc(soft_step[l][4], 1)

            def soft_inverses(l, g):
                dve.wait_ge(soft_step[l][4], g.done())
                dve.reciprocal(row[l][:, 7:9], row[l][:, 5:7]).then_inc(soft_step[l][5], 1)

            def soft_attn(l, g):
                dve.wait_ge(soft_step[l][5], g.done())
                if g.back(1).begun():
                    dve.wait_ge(attnT_done[l], g.back(1).done())
                dve.tensor_scalar(attn[l][:, :], masked[l][:, :], row[l][:, 7:8], P_SCALE, ALU.mult,
                                  ALU.mult).then_inc(soft_step[l][6], 1)

            def soft_diagonal(l, g):
                dve.tensor_tensor_reduce(diag_junk[l][:, :], masked[l][:, :], ident[:, :], 1.0, 0.0,
                                         ALU.mult, ALU.add, row[l][:, 3:4]).then_inc(soft_step[l][7], 1)

            def soft_factors(l, g):
                dve.wait_ge(soft_step[l][7], g.done())
                dve.tensor_tensor(row[l][:, 9:11], row[l][:, 3:5], row[l][:, 7:9], ALU.mult).then_inc(soft_step[l][8], 1)

            def soft_factor_squared(l, g):
                dve.wait_ge(soft_step[l][8], g.done())
                dve.tensor_tensor(row[l][:, 11:12], row[l][:, 10:11], row[l][:, 10:11], ALU.mult).then_inc(soft_step[l][9], 1)

            def side_values(l, side, g):
                w = (LEFT, RIGHT)[side]
                dve.wait_ge(val_done[l][w], g.done())
                if g.back(1).begun():
                    dve.wait_ge(val_lo_made[l][side], g.back(1).done())
                dve.scalar_tensor_tensor(val[l][:, side, :], val_ps[l][w][:, 0:D], VAL_SCALE, bd[:, l, w, :],
                                         ALU.mult, ALU.add).then_inc(val_made[l][side], 1)

            def attn_sides(l, g):
                dve.wait_ge(attnT_done[l], g.done())
                if g.back(1).begun():
                    dve.wait_ge(sides_lo_made[l], g.back(1).done())
                dve.tensor_tensor(sides[l][:, :, :], attnT_ps[l].unsqueeze(1).broadcast_to([128, 2, 128]),
                                  side_mask[:, :, :], ALU.mult).then_inc(sides_made[l], 1)

            def digcn_ctx(l, g):
                dve.wait_ge(soft_step[l][8], g.done())
                dve.wait_ge(self_made[l], g.done())
                dve.wait_ge(ctx_done[l], g.done())
                dve.scalar_tensor_tensor(ctx_sb[l][:, :], self_val[l][:, :], row[l][:, 9:10], ctx_ps[l][:, 0:D],
                                         ALU.mult, ALU.add).then_inc(ctx_step[l][0], 1)

            def digcn_sums(l, g):
                dve.wait_ge(ctx_step[l][0], g.done())
                sums_of(ctx_sb[l][:, :], 1 + l, ctx_step[l][1])

            def digcn_var(l, g):
                dve.wait_ge(ctx_step[l][2], g.done())
                dve.wait_ge(soft_step[l][9], g.done())
                dve.tensor_scalar(var2[1 + l][:, :], mean_var[1 + l][:, 1:2], row[l][:, 11:12], eps_l[l],
                                  ALU.mult, ALU.add).then_inc(ctx_step[l][3], 1)

            def digcn_centre(l, g):
                dve.scalar_tensor_tensor(ln_t[l][:, :], ctx_sb[l][:, :], mean_var[1 + l][:, 0:1], lnw[:, l, :],
                                         ALU.subtract, ALU.mult).then_inc(ctx_step[l][4], 1)

            def digcn_factor(l, g):
                dve.wait_ge(rstd_made[1 + l], g.done())
                dve.wait_ge(soft_step[l][8], g.done())
                dve.tensor_tensor(row[l][:, 12:13], rstd[1 + l][:, :], row[l][:, 10:11], ALU.mult).then_inc(ctx_step[l][5], 1)

            def digcn_norm(l, g):
                dve.wait_ge(ctx_step[l][5], g.done())
                if l == 0:
                    if g.back(1).begun():
                        dve.wait_ge(tr_done[1], g.back(1).done())
                dst = h_nat[1] if l == 0 else ln_out
                dve.scalar_tensor_tensor(dst[:, :], ln_t[l][:, :], row[l][:, 12:13], lnb[:, l, :], ALU.mult,
                                         ALU.add).then_inc(ctx_step[l][6], 1)

            def residual(g):
                dve.wait_ge(ctx_step[1][6], g.done())
                if g.back(1).begun():
                    dve.wait_ge(x1_bo_made, g.back(1).done())
                dve.scalar_tensor_tensor(x1[:, :], ln_out[:, :], 0.0, x_in[:, g.parity, :], ALU.max,
                                         ALU.add).then_inc(res_step[0], 1)

            def residual_sums(g):
                dve.wait_ge(res_step[0], g.done())
                sums_of(x1[:, :], 3, res_step[1])

            def qk_lo(n, g):
                ps, hi, lo, s = ((q_ps, q_hi, q_lo, SCALE * 2.0 ** -15), (k_ps, k_hi, k_lo, VAL_SCALE))[n]
                dve.wait_ge(qk_hi_made[n], g.done())
                dve.scalar_tensor_tensor(lo[:, :, :], ps[:, 0:D].rearrange("p (c n) -> p c n", c=C), s, hi[:, :, :],
                                         ALU.mult, ALU.subtract).then_inc(qk_lo_made[n], 1)

            def v_biased(g):
                dve.wait_ge(v_done, g.done())
                if g.back(1).begun():
                    dve.wait_ge(v_lo_made, g.back(1).done())
                dve.scalar_tensor_tensor(v_sb[:, :], v_ps[:, 0:D], VAL_SCALE, bv_b[:, :], ALU.mult,
                                         ALU.add).then_inc(v_made, 1)

            def head_scores(r, g):
                dve.wait_ge(s_done, g.at(R, r + 1))
                if r == 0:
                    dve.wait_ge(adj_scaled, g.done())
                    if g.back(1).begun():
                        dve.wait_ge(prob_made, g.back(1).at(R, R))
                        dve.wait_ge(pad_step[1], g.back(1).done())
                apart(dve, 4 + r)
                for c in range(C):
                    ins = dve.tensor_tensor_reduce(score_neg[:, r, c, :], s_ps[r][:, c * 128:(c + 1) * 128], adj_s[:, :],
                                                   s_scale_neg, HIGHEST, ALU.add, ALU.min, top_neg[:, r, c:c + 1])
                ins.then_inc(score_made, 1)

            flat = "p r c -> p (r c)"

            def top_not_zero(g):
                dve.wait_ge(score_made, g.at(R, R))
                dve.tensor_scalar(top_nonzero[:, :], top_neg[:, :, :].rearrange(flat), 0.0, None,
                                  ALU.not_equal).then_inc(pad_step[0], 1)

            def pad_kept(g):
                dve.wait_ge(score_summed, g.at(R, R))
                dve.wait_ge(pad_step[0], g.done())
                dve.scalar_tensor_tensor(kept[:, :, :].rearrange(flat), score_sum[:, :, :].rearrange(flat), 0.0,
                                         top_nonzero[:, :], ALU.not_equal, ALU.max).then_inc(pad_step[1], 1)

            pv = pv_ps.rearrange("p (h d) -> p h d", h=H)

            def inverse_sums(g):
                dve.wait_ge(pv_done, g.done())
                dve.reciprocal(inv_sum[:, :].unsqueeze(2), pv[:, :, HD:HD + 1]).then_inc(o_step[0], 1)

            def inverse_kept(g):
                dve.wait_ge(o_step[0], g.done())
                dve.wait_ge(pad_step[1], g.done())
                dve.tensor_tensor(inv_kept[:, :].rearrange("p (c r) -> p c r", c=C),
                                  inv_sum[:, :].rearrange("p (c r) -> p c r", c=C),
                                  kept[:, :, :].rearrange("p r c -> p c r"), ALU.mult).then_inc(o_step[1], 1)

            def head_outputs(g):
                dve.wait_ge(o_step[1], g.done())
                if g.back(1).begun():
                    dve.wait_ge(oT_done, g.back(1).done())
                dve.tensor_tensor(o_nat[:, :].rearrange("p (h d) -> p h d", h=H), pv[:, :, 0:HD],
                                  inv_kept[:, :].unsqueeze(2).broadcast_to([128, H, HD]), ALU.mult).then_inc(o_step[2], 1)

            def oT_lo_of(g):
                dve.wait_ge(oT_hi_made, g.done())
                dve.tensor_tensor(oT_lo[:, :, :], oT_ps.rearrange("p (c n) -> p c n", c=C), oT_hi[:, :, :],
                                  ALU.subtract).then_inc(oT_lo_made, 1)

            def step(t):
                g1, g2, nxt = t.back(1), t.back(2), t.back(-1)
                if t.exists():
                    soft_max(0, t)
                if g1.exists():
                    digcn_centre(1, g1)
                if t.exists():
                    soft_max_scaled(0, t)
                if g1.exists():
                    digcn_factor(1, g1)
                    digcn_norm(1, g1)
                if t.exists():
                    soft_masked(0, t)
                    side_values(0, 0, t)
                    soft_sums(0, t)
                if g1.exists():
                    residual(g1)
                if t.exists():
                    soft_inverses(0, t)
                if g1.exists():
                    residual_sums(g1)
                if t.exists():
                    soft_attn(0, t)
                    if t.first():
                        split_low(3)
                if g1.exists():
                    mean_var_of(3, res_step[1], res_step[2], g1)
                if t.exists():
                    side_values(0, 1, t)
                if g1.exists():
                    outer_var(3, res_step[2], res_step[3], g1)
                if g2.exists():
                    top_not_zero(g2)
                if t.exists():
                    attn_sides(0, t)
                    if t.first():
                        split_low(4)
                    soft_diagonal(0, t)
                    if t.first():
                        split_low(5)
                if g1.exists():
                    normalise(x1[:, :], 3, 2, res_step[4], g1)
                if g2.exists():
                    v_biased(g2)
                if t.exists():
                    soft_factors(0, t)
                if nxt.exists():
                    input_sums(nxt)
                if g1.exists():
                    hT_lo_of(2, g1)
                if t.exists():
                    digcn_ctx(0, t)
                    digcn_sums(0, t)
                    soft_factor_squared(0, t)
                    mean_var_of(1, ctx_step[0][1], ctx_step[0][2], t)
                    digcn_var(0, t)
                if nxt.exists():
                    mean_var_of(0, ln0_step[0], ln0_step[1], nxt)
                if t.exists():
                    digcn_centre(0, t)
                    digcn_factor(0, t)
                    digcn_norm(0, t)
                if g2.exists():
                    pad_kept(g2)
                if nxt.exists():
                    outer_var(0, ln0_step[1], ln0_step[2], nxt)
                if g1.exists():
                    qk_lo(0, g1)
                    qk_lo(1, g1)
                if t.exists():
                    hT_lo_of(1, t)
                    if t.first():
                        split_low(6)
                if nxt.exists():
                    normalise(x_in[:, nxt.parity, :], 0, 0, ln0_step[3], nxt)
                if g1.exists():
                    head_scores(0, g1)
                if t.exists():
                    soft_max(1, t)
                    if t.first():
                        split_low(7)
                if g2.exists():
                    inverse_sums(g2)
                if t.exists():
                    soft_max_scaled(1, t)
                if g2.exists():
                    inverse_kept(g2)
                    head_outputs(g2)
                if t.exists():
                    soft_masked(1, t)
                    soft_sums(1, t)
                    side_values(1, 0, t)
                    soft_inverses(1, t)
                    soft_attn(1, t)
                    if t.first():
                        split_low(8)
                    soft_diagonal(1, t)
                    side_values(1, 1, t)
                    attn_sides(1, t)
                    if t.first():
                        split_low(9)
                    soft_factors(1, t)
                if g1.exists():
                    head_scores(1, g1)
                    head_scores(2, g1)
                if g2.exists():
                    oT_lo_of(g2)
                if nxt.exists():
                    hT_lo_of(0, nxt)
                if g1.exists():
                    head_scores(3, g1)
                if t.exists():
                    digcn_ctx(1, t)
                    soft_factor_squared(1, t)
                    digcn_sums(1, t)
                    mean_var_of(2, ctx_step[1][1], ctx_step[1][2], t)
                    digcn_var(1, t)

            g0 = Graph(0, 0, B - 1)
            input_sums(g0)
            mean_var_of(0, ln0_step[0], ln0_step[1], g0)
            outer_var(0, ln0_step[1], ln0_step[2], g0)
            normalise(x_in[:, 0, :], 0, 0, ln0_step[3], g0)
            def weight_max(n):
                dve.wait_ge(weight_in[n], 16)
                absmax(bounds[:, n:n + 1], weight(wd_raw, wm_raw, n).rearrange("p c e -> p (c e)")).then_inc(bounds_made, 1)

            for n in range(3):
                weight_max(n)
            dve.wait_ge(spread_in, 16 * len(spread))
            for n, tile in enumerate(spread_tiles):
                absmax(bias_part[:, n:n + 1], tile[:, :]).then_inc(bias_bounds_made, 1)
            for n in range(3, 5):
                weight_max(n)
            hT_lo_of(0, g0)
            dve.wait_ge(consts_made, 9)
            dve.wait_ge(bias_bounds_shared, 1)
            own(dve.tensor_tensor(h_need[:, :], bias_max[:, 3:4], bias_max[:, 4:5], ALU.add))
            own(dve.tensor_scalar(h_need[:, :], h_need[:, :], SMALLEST, None, ALU.max))
            inverse_power_of_two(tmp_a, tmp_b, h_need[:, :])
            own(dve.tensor_scalar(s_h1, tmp_a, H_SCALE / 2, None, ALU.mult))
            own(dve.tensor_scalar(ratio1, s_h1, 1.0 / (H_SCALE * D), None, ALU.mult))
            dve.tensor_scalar(least[:, 0:1], bias_max[:, 0:1], 1.0 / D, SMALLEST, ALU.mult, ALU.max)
            own(dve.tensor_tensor(tmp_a, bias_max[:, 1:2], ratio1, ALU.mult))
            dve.tensor_scalar(least[:, 1:2], tmp_a, SMALLEST, None, ALU.max)
            own(dve.tensor_scalar(least[:, 4:5], bias_max[:, 2:3], 1.0 / D, SMALLEST, ALU.mult, ALU.max))
            own(dve.tensor_tensor(tmp_a, s_h1, s_h1, ALU.mult))
            own(dve.reciprocal(tmp_b, tmp_a))
            own(dve.tensor_scalar(u_scale1, tmp_b, SCALE, None, ALU.mult))
            for n in range(5, n_weights):
                weight_max(n)
            dve.wait_ge(bounds_shared, 1)
            dve.tensor_reduce(need[:, 0:L], bound_all[:, 0:3 * L].rearrange("p (l w) -> p l w", l=L), X_AXIS, ALU.max)
            own(dve.tensor_copy(need[:, L:L + 4], bound_all[:, 3 * L:n_weights]))
            own(dve.tensor_tensor(need[:, :], need[:, :], least[:, :], ALU.max))
            inverse_power_of_two(inv2[:, :], pow2[:, :], need[:, :])
            dve.tensor_scalar(scl[:, 0:L + 4], inv2[:, :], W_TOP, None, ALU.mult).then_inc(scales_made, 1)
            dve.wait_ge(scales_made, 1)
            dve.tensor_scalar(val0, s_w0, H_SCALE * VAL_SCALE, None, ALU.mult)
            dve.tensor_scalar(val_v, s_v, H_SCALE * VAL_SCALE, None, ALU.mult)
            own(dve.tensor_scalar(val1, s_w1, VAL_SCALE, None, ALU.mult))
            own(dve.tensor_tensor(val1, val1, s_h1, ALU.mult))
            for n in range(3):
                split_low(n)
            for l in range(L):
                dve.tensor_scalar(eps_l[l], val_scale[l], P_SCALE * DIGCN_EPS ** 0.5, None, ALU.mult)
            own(dve.tensor_scalar(tmp_a, s_q, 2.0 ** -14, None, ALU.mult))
            for l in range(L):
                dve.tensor_tensor(eps_l[l], eps_l[l], eps_l[l], ALU.mult)
            own(dve.tensor_tensor(adj_scale, tmp_a, s_k, ALU.mult))
            own(dve.tensor_tensor(tmp_b, val_v, s_o, ALU.mult))
            own(dve.tensor_scalar(tmp_a, adj_scale, -1.0, None, ALU.mult))
            dve.reciprocal(s_scale_neg, tmp_a)
            dve.reciprocal(out_scale, tmp_b)
            dve.wait_ge(small_in, 16 * n_small)
            dve.tensor_scalar(lnw[:, 0, :], lnw[:, 0, :], s_h1, None, ALU.mult)
            dve.tensor_scalar(lnb[:, 0, :], lnb[:, 0, :], s_h1, None, ALU.mult)
            for l in range(L):
                for w in (LEFT, RIGHT):
                    dve.tensor_scalar(bd[:, l, w, :], bd[:, l, w, :], val_scale[l], None, ALU.mult)
                dve.tensor_scalar(bd[:, l, SELF, :], bd[:, l, SELF, :], val_scale[l], P_SCALE, ALU.mult, ALU.mult)
            dve.tensor_scalar(bv_b[:, :], bv_b[:, :], val_v, None, ALU.mult).then_inc(prepared, 1)
            dve.wait_ge(prepared, 1)
            run_pipeline(dve, step)

        @block.tensor
        def _(pe):
            def three(out_ap, a_hi, a_lo, b_hi, b_lo, first, last):
                pe.matmul(out_ap, a_hi, b_hi, start=first, stop=False)
                pe.matmul(out_ap, a_hi, b_lo, start=False, stop=False)
                return pe.matmul(out_ap, a_lo, b_hi, start=False, stop=last)

            def transposes(s, made, g):
                pe.wait_ge(made, g.done())
                for c in range(C):
                    ins = pe.transpose(t_ps[s][:, c * 128:(c + 1) * 128], h_nat[s][:, c * 128:(c + 1) * 128], ident[:, :])
                ins.then_inc(tr_done[s], 1)

            def graph_scores(l, g):
                for c in range(C):
                    hi, lo = hT_hi[l][:, c, :], hT_lo[l][:, c, :]
                    ins = three(u_ps[l], hi, lo, hi, lo, c == 0, c == C - 1)
                ins.then_inc(u_done[l], 1)

            def node_values(l, w, g):
                if g.first():
                    pe.wait_ge(w_split_lo, 3 * l + w + 1)
                for c in range(C):
                    ins = three(val_ps[l][w][:, 0:D], hT_hi[l][:, c, :], hT_lo[l][:, c, :], wd_hi[:, l, w, c, :],
                                wd_lo[:, l, w, c, :], c == 0, c == C - 1)
                ins.then_inc(val_done[l][w], 1)

            def transpose_attn(l, g):
                pe.wait_ge(soft_step[l][6], g.done())
                pe.transpose(attnT_ps[l], attn[l][:, :], ident[:, :]).then_inc(attnT_done[l], 1)

            def weigh_values(l, g):
                pe.wait_ge(sides_lo_made[l], g.done())
                for side in range(2):
                    pe.wait_ge(val_lo_made[l][side], g.done())
                    ins = three(ctx_ps[l][:, 0:D], sides_hi[l][:, side, :], sides_lo[l][:, side, :],
                                val_hi[l][:, side, :], val_lo[l][:, side, :], side == 0, side == 1)
                ins.then_inc(ctx_done[l], 1)

            def project_qk(n, g):
                if g.first():
                    pe.wait_ge(w_split_lo, 3 * L + n + 1)
                pe.wait_ge(hT_lo_made[2], g.done())
                ps = (q_ps, k_ps)[n]
                for e in range(C):
                    cols = slice(e * 128, (e + 1) * 128)
                    for c in range(C):
                        ins = three(ps[:, cols], wm_hi[:, n, c, cols], wm_lo[:, n, c, cols],
                                    hT_hi[2][:, c, :], hT_lo[2][:, c, :], c == 0, c == C - 1)
                ins.then_inc(qk_done[n], 1)

            def head_scores(r, g):
                pe.wait_ge(qk_lo_made[0], g.at(1, 1))
                pe.wait_ge(qk_lo_made[1], g.at(1, 1))
                rows = slice(r * HD, (r + 1) * HD)
                for c in range(C):
                    ins = three(s_ps[r][:, c * 128:(c + 1) * 128], q_hi[rows, c, :], q_lo[rows, c, :],
                                k_hi[rows, c, :], k_lo[rows, c, :], True, True)
                ins.then_inc(s_done, 1)

            def transpose_probs(b, g):
                for a in range(R):
                    r, c = divmod(b * R + a, C)
                    if a == 0 or c == 0:
                        pe.wait_ge(prob_made, g.at(R, r + 1))
                    ins = pe.transpose(pT_ps[b][:, a * 128:(a + 1) * 128], prob[:, r, c, :], ident[:, :])
                ins.then_inc(pT_done, 1)

            def weigh_by_probs(g):
                pe.wait_ge(v_lo_made, g.done())
                for b in range(C):
                    pe.wait_ge(pT_lo_made, g.at(C, b + 1))
                    for a in range(R):
                        r, c = divmod(b * R + a, C)
                        h = c * R + r
                        ins = three(pv_ps[:, h * (HD + 1):(h + 1) * (HD + 1)], pT_hi[:, b, a, :], pT_lo[:, b, a, :],
                                    v_hi[:, h, :], v_lo[:, h, :], True, True)
                ins.then_inc(pv_done, 1)

            def transpose_o(g):
                pe.wait_ge(o_step[2], g.done())
                for c in range(C):
                    ins = pe.transpose(oT_ps[:, c * 128:(c + 1) * 128], o_nat[:, c * 128:(c + 1) * 128], ident[:, :])
                ins.then_inc(oT_done, 1)

            def project_v(g):
                if g.first():
                    pe.wait_ge(w_split_lo, 3 * L + WV + 1)
                for c in range(C):
                    ins = three(v_ps[:, 0:D], hT_hi[2][:, c, :], hT_lo[2][:, c, :], wm_hi[:, WV, c, :],
                                wm_lo[:, WV, c, :], c == 0, c == C - 1)
                ins.then_inc(v_done, 1)

            def project_out(g):
                if g.first():
                    pe.wait_ge(w_split_lo, 3 * L + WO + 1)
                pe.wait_ge(oT_lo_made, g.done())
                for c in range(C):
                    ins = three(wo_ps, oT_hi[:, c, :], oT_lo[:, c, :], wm_hi[:, WO, c, :], wm_lo[:, WO, c, :],
                                c == 0, c == C - 1)
                ins.then_inc(wo_done, 1)

            def step(t):
                g1, g2, nxt = t.back(1), t.back(2), t.back(-1)
                if t.exists():
                    if t.back(3).exists():
                        pe.wait_ge(oT_lo_made, t.back(3).done())
                    elif g2.exists():
                        pe.wait_ge(qk_lo_made[0], g2.done())
                    elif g1.exists():
                        pe.wait_ge(exp_done[0], g1.done())
                    pe.wait_ge(hT_lo_made[0], t.done())
                    graph_scores(0, t)
                if g2.exists():
                    pe.wait_ge(qk_lo_made[1], g2.done())
                    transpose_probs(0, g2)
                if t.exists():
                    if g1.exists():
                        pe.wait_ge(val_made[1][1], g1.done())
                    node_values(0, LEFT, t)
                    if g2.exists():
                        pe.wait_ge(score_made, g2.at(R, 4))
                    elif g1.exists():
                        pe.wait_ge(val_made[0][1], g1.done())
                    node_values(0, RIGHT, t)
                    if t.back(3).exists():
                        pe.wait_ge(out_scaled, t.back(3).done())
                    elif g1.exists():
                        pe.wait_ge(self_copied[1], g1.done())
                    node_values(0, SELF, t)
                    if g2.exists():
                        pe.wait_ge(pT_copied, g2.at(C, 1))
                    elif g1.exists():
                        pe.wait_ge(sides_made[0], g1.done())
                    transpose_attn(0, t)
                if g2.exists():
                    if t.exists():
                        pe.wait_ge(val_made[0][1], t.done())
                    else:
                        pe.wait_ge(score_made, g2.at(R, 4))
                    project_v(g2)
                if g1.exists():
                    if t.exists():
                        pe.wait_ge(hT_lo_made[0], t.done())
                    else:
                        pe.wait_ge(val_made[1][0], g1.done())
                    transposes(2, res_step[4], g1)
                if g2.exists():
                    if t.exists():
                        pe.wait_ge(self_copied[0], t.done())
                    elif t.back(3).exists():
                        pe.wait_ge(out_scaled, t.back(3).done())
                    transpose_probs(1, g2)
                if t.exists():
                    if g1.exists():
                        pe.wait_ge(ctx_step[1][0], g1.done())
                    weigh_values(0, t)
                if g2.exists():
                    pe.wait_ge(v_made, g2.done())
                    transpose_probs(2, g2)
                if g1.exists():
                    if t.exists():
                        pe.wait_ge(exp_done[0], t.done())
                    elif t.back(3).exists():
                        pe.wait_ge(oT_lo_made, t.back(3).done())
                    project_qk(0, g1)
                    if t.exists():
                        pe.wait_ge(sides_made[0], t.done())
                    elif g2.exists():
                        pe.wait_ge(pT_copied, g2.at(C, 1))
                    project_qk(1, g1)
                if t.exists():
                    pe.wait_ge(ctx_step[0][0], t.done())
                    transposes(1, ctx_step[0][6], t)
                if g2.exists():
                    pe.wait_ge(pT_copied, g2.at(C, 2))
                    weigh_by_probs(g2)
                if g1.exists():
                    if t.exists():
                        pe.wait_ge(val_made[0][0], t.done())
                    else:
                        pe.wait_ge(val_made[1][1], g1.done())
                    head_scores(0, g1)
                    if g2.exists():
                        pe.wait_ge(pT_copied, g2.at(C, 3))
                    elif t.exists():
                        pe.wait_ge(val_made[0][1], t.done())
                    head_scores(1, g1)
                if t.exists():
                    if g1.exists():
                        pe.wait_ge(exp_done[1], g1.done())
                    pe.wait_ge(hT_lo_made[1], t.done())
                    graph_scores(1, t)
                    if g1.exists():
                        pe.wait_ge(hT_lo_made[2], g1.done())
                    else:
                        pe.wait_ge(hT_lo_made[0], t.done())
                    node_values(1, LEFT, t)
                    if g1.exists():
                        pe.wait_ge(score_made, g1.at(R, 1))
                    else:
                        pe.wait_ge(val_made[0][0], t.done())
                    node_values(1, RIGHT, t)
                if g2.exists():
                    if g1.exists():
                        pe.wait_ge(qk_lo_made[0], g1.done())
                    elif t.back(3).exists():
                        pe.wait_ge(oT_lo_made, t.back(3).done())
                    transpose_o(g2)
                if t.exists():
                    if g2.exists():
                        pe.wait_ge(o_step[2], g2.done())
                    else:
                        pe.wait_ge(self_copied[0], t.done())
                    transpose_attn(1, t)
                if g1.exists():
                    if t.exists():
                        pe.wait_ge(hT_lo_made[1], t.done())
                    else:
                        pe.wait_ge(ctx_step[1][0], g1.done())
                    head_scores(2, g1)
                if nxt.exists():
                    pe.wait_ge(val_made[1][0], t.done())
                    transposes(0, ln0_step[3], nxt)
                if t.exists():
                    pe.wait_ge(sides_made[1], t.done())
                    node_values(1, SELF, t)
                if g1.exists():
                    pe.wait_ge(score_made, g1.at(R, 2))
                    head_scores(3, g1)
                if t.exists():
                    if g1.exists():
                        pe.wait_ge(score_made, g1.at(R, 3))
                    else:
                        pe.wait_ge(hT_lo_made[1], t.done())
                    weigh_values(1, t)
                if g2.exists():
                    if t.exists():
                        pe.wait_ge(self_copied[1], t.done())
                    else:
                        pe.wait_ge(o_step[2], g2.done())
                    project_out(g2)

            pe.wait_ge(consts_made, 9)
            transposes(0, ln0_step[3], Graph(0, 0, B - 1))
            run_pipeline(pe, step)


_OUT = ((128, 128, 384), "float32")


def kernel(**inputs):
    import numpy as _np
    import concourse.bacc as _bacc
    from concourse import mybir as _mybir
    from concourse.bass_utils import run_bass_kernel_spmd as _run

    a = {k: _np.asarray(v) for k, v in inputs.items()}
    arrays = {
        "x": a["x"],
        "adj": a["adj"],
        "w_digcn": _np.stack([a["L0_gnn_Wl"], a["L0_gnn_Ws"], a["L0_gnn_Wr"]], axis=1).transpose(0, 1, 3, 2),
        "b_digcn": _np.stack([a["L0_gnn_bl"], a["L0_gnn_bs"], a["L0_gnn_br"]], axis=1),
        "ln_w": a["L0_gnn_ln_w"],
        "ln_b": a["L0_gnn_ln_b"],
        "w_mha": _np.stack([a["L1_gnn_Wq"], a["L1_gnn_Wk"], a["L1_gnn_Wv"], a["L1_gnn_Wo"]]).transpose(0, 2, 1),
        "bv": a["L1_gnn_bv"],
        "bo": a["L1_gnn_bo"],
    }
    arrays = {f"in_{k}": _np.ascontiguousarray(v) for k, v in arrays.items()}
    nc = _bacc.Bacc("TRN2", target_bir_lowering=False, num_devices=1)
    args = [nc.dram_tensor(k, v.shape, _mybir.dt.from_np(v.dtype), kind="ExternalInput").ap() for k, v in arrays.items()]
    shape, dtype = _OUT
    res = nc.dram_tensor("out_0", shape, _mybir.dt.from_np(_np.dtype(dtype)), kind="ExternalOutput").ap()
    two_gnn_blocks(nc, *args, res)
    r = _run(nc, [arrays], core_ids=[0])
    return r.results[0]["out_0"]
```
